# Optimizing a Trainium2 kernel written in Bass

```python
import numpy as np
import jax
import jax.numpy as jnp

def _softmax(x, axis=-1):
    return jax.nn.softmax(x, axis=axis)
def _gelu(x):
    return jax.nn.gelu(x, approximate=True)
def _silu(x):
    return jax.nn.silu(x)
def _sigmoid(x):
    return jax.nn.sigmoid(x)
def _layernorm(x, axis=-1, eps=1e-5):
    m = jnp.mean(x, axis=axis, keepdims=True)
    v = jnp.var(x, axis=axis, keepdims=True)
    return (x - m) / jnp.sqrt(v + eps)
def _scatter_add(tgt, idx, src, axis=0):
    return tgt.at[idx].add(src)
def _segment_sum(src, seg, n):
    return jax.ops.segment_sum(src, seg, n)

kernel_name = 'mk_adj_resnorm_d2_adj_128_87fd44'

def setup_inputs(seed: int = 0):
    np.random.seed(seed)
    _w = jnp.asarray
    def _rec_inputs():
        import jax
        import jax.numpy as jnp
        _gk = jax.random.key(seed)
        x = 0.0002279 + 0.9999 * jax.random.normal(jax.random.fold_in(_gk, 1), (8192, 128), jnp.float32)
        _a = jax.random.bernoulli(jax.random.fold_in(_gk, 2), 0.00195312, (8192, 8192))
        _a = jnp.logical_or(_a, jnp.swapaxes(_a, -1, -2))
        _a = jnp.logical_or(_a, jnp.eye(8192, dtype=bool))
        adj = _a.astype(jnp.int32)
        return x, adj
    x, adj = _rec_inputs()
    def _L0_gnn_setup():
        import jax, jax.numpy as jnp
        import numpy as np
        N, D = (8192, 128)
        key = jax.random.key(seed)
        k1, k2, k3 = jax.random.split(key, 3)
        adj = jax.random.randint(k1, (N, N), 0, 2, dtype=jnp.int32)
        emb = jax.random.normal(k2, (N, D), dtype=jnp.float32)
        attn = jax.random.normal(k3, (2 * D, 1), dtype=jnp.float32)
        return {'adj': adj, 'emb': emb, 'attn': attn}
    _L0_gnn_all = _L0_gnn_setup()
    _L0_gnn_in = {k: v for k, v in _L0_gnn_all.items() if k in ('attn', )}
    del _L0_gnn_all

    def _L1_gnn_setup():
        import jax
        import jax.numpy as jnp
        import numpy as np
        from jax import lax
        N = 8192
        F = 128
        CHUNK = 64
        key = jax.random.key(seed)
        kx, ka = jax.random.split(key)
        X = jax.random.normal(kx, (N, F), dtype=jnp.float32)
        adj = jax.random.randint(ka, (N, N), 0, 2, dtype=jnp.int32)
        return {'X': X, 'adj': adj}
    _L1_gnn_all = _L1_gnn_setup()
    _L1_gnn_in = {k: v for k, v in _L1_gnn_all.items() if k in ()}
    del _L1_gnn_all

    return {
        "x": x,
        "adj": adj,
        "L0_gnn_attn": _L0_gnn_in["attn"],
    }

def reference(x, adj, L0_gnn_attn):
    import jax
    import jax.numpy as jnp
    def _L0_gnn_ref(adj, emb, attn):
        import jax, jax.numpy as jnp
        import numpy as np
        N, D = (8192, 128)
        d = emb.shape[1]
        s_i = emb @ attn[:d]
        s_j = emb @ attn[d:]
        e = jax.nn.leaky_relu(s_i + s_j.T, negative_slope=0.2)
        neg_inf = jnp.float32(-1000000000.0)
        e = e + jnp.where(adj > 0, jnp.float32(0.0), neg_inf)
        alpha = jax.nn.softmax(e, axis=1)
        return alpha @ emb

    def _L1_gnn_ref(X, adj):
        import jax
        import jax.numpy as jnp
        import numpy as np
        from jax import lax
        N = 8192
        F = 128
        CHUNK = 64
        neg = jnp.finfo(X.dtype).min
        mask = adj != 0
        n, f = X.shape

        def body(_, mrows):
            vals = jnp.max(jnp.where(mrows[:, :, None], X[None, :, :], neg), axis=1)
            has_nbr = jnp.any(mrows, axis=1)
            return (None, jnp.where(has_nbr[:, None], vals, jnp.zeros((), X.dtype)))
        _, out = lax.scan(body, None, mask.reshape(n // CHUNK, CHUNK, n))
        return out.reshape(n, f)

    x = _layernorm(x + _L0_gnn_ref(adj, x, L0_gnn_attn), axis=-1)
    x = _layernorm(x + _L1_gnn_ref(x, adj), axis=-1)
    return x


_drawn_inputs = setup_inputs


def setup_inputs(seed=0):
    import zlib

    import numpy as np

    out = dict(_drawn_inputs(seed))
    spreads = {}
    factors = {}
    for name, (base, spread) in spreads.items():
        noise = np.random.default_rng([zlib.crc32(name.encode()), seed]).standard_normal(out[name].shape)
        drawn = base * np.exp(spread * noise) if base else spread * noise
        out[name] = jnp.asarray(drawn.astype(out[name].dtype))
    for name, factor in factors.items():
        out[name] = (out[name] * factor).astype(out[name].dtype)
    return out
```

```python
import numpy as np
import concourse.bass as bass
from concourse import mybir
from contextlib import ExitStack

F32 = mybir.dt.float32
I32 = mybir.dt.int32
U32 = mybir.dt.uint32
I16 = mybir.dt.int16
ALU = mybir.AluOpType
ACT = mybir.ActivationFunctionType
AX = mybir.AxisListType

P = 128
SLOTS = 64
CH = 4
BASE_CH = 6
SEG = 128
GT = 8
LAG = 10
SLOPE, NEG, EPS = 0.2, -1e9, 1e-5
FAR = -3.0e38
DENSE_CH = 64


def gnn_kernel(nc, x, adj, attn, out):
    N, D = x.shape
    NT = N // P
    NG = NT // GT
    H = N // 2
    NSEG = N // SEG
    NCH = SLOTS // CH
    TCOL, SCOL, XW = D, D + 1, D + 4
    DEG, OWN, XAT = SLOTS, SLOTS + 1, SLOTS + 4
    LW = XAT + XW
    HEAD = 3 * NSEG
    ND = N // DENSE_CH

    xs = nc.dram_tensor("xs", [N, XW], F32).ap()
    trow = nc.dram_tensor("trow", [N], F32).ap()
    x1 = nc.dram_tensor("x1", [N, D], F32).ap()
    lists = nc.dram_tensor("lists", [N, LW], U32).ap()

    with ExitStack() as ctx:
        def sb(name, shape, dt):
            return ctx.enter_context(nc.sbuf_tensor(name, shape, dt))

        def sem(name):
            return ctx.enter_context(nc.semaphore(name))

        adjb = sb("adjb", [P, 2, H], I32)
        nz = sb("nz", [P, 2, N], I16)
        iota16 = sb("iota16", [P, N], I16)
        G = sb("G", [P, 2, SLOTS, XW], F32)
        x1keep = sb("x1keep", [P, NT, D], F32)
        lists_g = sb("lists_g", [P, GT, LW], U32)
        lp = sb("lp", [P, 2, LW], U32)
        comb = sb("comb", [P, 8 + 8 * NSEG], F32)
        found_l = sb("found_l", [P, SLOTS], F32)
        fill = sb("fill", [P, SLOTS], F32)
        junk = sb("junk", [P, SLOTS], F32)
        halves = sb("halves", [P, 2, 2], F32)
        count = sb("count", [P, 1], F32)
        found = sb("found", [P, GT], F32)
        miss = sb("miss", [P, 2], F32)
        bad = sb("bad", [P, NT], F32)
        key = sb("key", [P, GT], F32)
        order_c = sb("order_c", [P, GT], F32)
        own_c = sb("own_c", [P, GT], F32)
        rank = sb("rank", [P, GT], F32)
        rank0 = sb("rank0", [P, GT], F32)
        place = sb("place", [P, GT], U32)
        gbase = sb("gbase", [P, 1], F32)
        diag = sb("diag", [P, GT, P], F32)
        ident = sb("ident", [P, P], F32)
        ones = sb("ones", [P, P], F32)
        slot_no = sb("slot_no", [P, SLOTS], F32)
        attn_b = sb("attn_b", [P, 2 * D], F32)
        st = sb("st", [P, NT, 4], F32)
        stj = sb("stj", [P, D], F32)
        degf = sb("degf", [P, 2], F32)
        hide = sb("hide", [P, SLOTS], F32)
        z = sb("z", [P, SLOTS], F32)
        e = sb("e", [P, SLOTS], F32)
        nmax = sb("nmax", [P, 2], F32)
        w = sb("w", [P, 2, SLOTS], F32)
        wsum = sb("wsum", [P, 2], F32)
        wsafe = sb("wsafe", [P, 1], F32)
        wrec = sb("wrec", [P, 1], F32)
        acc = sb("acc", [P, CH, D], F32)
        agg = sb("agg", [P, D], F32)
        y = sb("y", [P, 2, D], F32)
        stats = sb("stats", [P, 6], F32)
        mv = sb("mv", [P, 2, 2], F32)
        root = sb("root", [P, 2], F32)
        rstd = sb("rstd", [P, 1], F32)
        rows_o = sb("rows_o", [P, 2, D], F32)
        own_o = sb("own_o", [P, 2, 2], U32)
        epsb = sb("epsb", [P, 1], F32)
        flags = sb("flags", [P, NT + 2], I32)
        flagf = sb("flagf", [P, NT + 2], F32)
        keys_ps = ctx.enter_context(nc.psum_tensor("keys_ps", [P, GT * P], F32))
        flag_ps = ctx.enter_context(nc.psum_tensor("flag_ps", [P, NT], F32))

        S = {n: sem(n) for n in (
            "x_in attn_in adj_in0 adj_in1 own_x lists_in0 lists_in1 gathered0 gathered1 gathered2 gathered3 "
            "iota_done ident_zero ident_done consts_done ones_done products dots st_zero xs_out g_zero signed squared "
            "segments tail_done picked replaced listed base_done diag_done keys_done ranked placed scattered "
            "step_a exped step_b rooted step_c fresh rows_scattered0 rows_scattered1 slot_done flags_mm flags_done "
            "out_scattered0 out_scattered1 "
            "pad_dve pad_pool pad_sp pad_act d_adj d_t d_own d_rows d_used d_stored d_pen d_exp d_var d_root d_fin").split()}
        adj_in = [S["adj_in0"], S["adj_in1"]]
        lists_in = [S["lists_in0"], S["lists_in1"]]
        gathered = [[S["gathered0"], S["gathered1"]], [S["gathered2"], S["gathered3"]]]

        def tile_rows(ap, t):
            return ap[bass.ds(t * P, P), :]

        rows_scattered = [S["rows_scattered0"], S["rows_scattered1"]]
        out_scattered = [S["out_scattered0"], S["out_scattered1"]]

        def held(eng, pad, s, value):
            eng.wait_ge(s, value)
            eng.sem_inc(S[pad], 1)

        def all_scattered(eng, sems):
            for b in range(2):
                eng.wait_ge(sems[b], 8 * NT)

        block = ctx.enter_context(nc.Block())


        E = G[:, 0, :, :].rearrange("p s w -> p (s w)")[:, 0:N]
        XB = G[:, 1, :, :].rearrange("p s w -> p (s w)")[:, 0:DENSE_CH * D]
        XBv = XB.rearrange("p (j d) -> p j d", d=D)
        penalty = adjb[:, :, :].rearrange("p a b -> p (a b)")
        xo = acc[:, 1, :]
        part = acc[:, 2, :]
        dacc = acc[:, 0, :]

        def dense_loads(sp, t, layer, base):
            n = t + base
            mark = sp.value_load(flags[0:1, bass.ds(t, 1)], min_val=0, max_val=P)
            src, dst = (x, x1) if layer == 0 else (x1, out)
            with sp.If(mark > 0):
                sp.dma_start(penalty, tile_rows(adj, t)).then_inc(S["d_adj"], 16)
                sp.dma_start(xo, tile_rows(src, t)).then_inc(S["d_own"], 16)
                if layer == 0:
                    sp.dma_start(E, trow.partition_broadcast(P)).then_inc(S["d_t"], 16)
                else:
                    sp.sem_inc(S["d_t"], 16)
                with sp.Fori(0, ND) as c:
                    sp.wait_ge(S["d_used"], n * ND + c)
                    sp.dma_start(XB, src[bass.ds(c * DENSE_CH, DENSE_CH), :]
                                 .rearrange("j d -> (j d)").partition_broadcast(P)).then_inc(S["d_rows"], 16)
            with sp.Else():
                for s, k in (("d_adj", 1), ("d_own", 1), ("d_t", 1), ("d_rows", ND)):
                    sp.sem_inc(S[s], 16 * k)
            held(sp, "pad_sp", S["d_fin"], n + 1)
            with sp.If(mark > 0):
                sp.dma_start(tile_rows(dst, t), rows_o[:, 0, :]).then_inc(S["d_stored"], 16)
            with sp.Else():
                sp.sem_inc(S["d_stored"], 16)
            held(sp, "pad_sp", S["d_stored"], 16 * (n + 1))

        @block.sync
        def _(sp):
            for h in range(2):
                sp.dma_start(adjb[:, h, :], adj[0:P, h * H:(h + 1) * H]).then_inc(adj_in[h], 16)
            sp.dma_start(x1keep[:, :, :], x.rearrange("(t p) d -> p t d", p=P)).then_inc(S["x_in"], 16)
            sp.dma_start(attn_b[:, :], attn.rearrange("d o -> (o d)").partition_broadcast(P))\
              .then_inc(S["attn_in"], 16)

            def load_lists(j, b):
                sp.dma_start(lp[:, b, :], tile_rows(lists, j)).then_inc(lists_in[b], 16)

            def next_half(i, h):
                sp.wait_ge(S["squared"], 2 * i + h + 1)
                sp.dma_start(adjb[:, h, :], tile_rows(adj, i + 1)[:, h * H:(h + 1) * H])\
                  .then_inc(adj_in[h], 16)

            def pair(i0, extract, layer, last=False):
                for u in range(2):
                    i = i0 + u
                    if extract and not (last and u == 1):
                        for h in range(2):
                            next_half(i, h)
                    if layer:
                        j = i - LAG
                        sp.wait_ge(S["step_b"], j + 1)
                        load_lists(j + 2, u)

            def own_x(g):
                sp.dma_start(lists_g[:, :, XAT:].bitcast(F32),
                             xs[bass.ds(g * GT * P, GT * P), :].rearrange("(t p) w -> p t w", p=P))\
                  .then_inc(S["own_x"], 16)

            sp.wait_ge(S["x_in"], 16)
            xs_v = xs.rearrange("(t p) w -> p t w", p=P)
            sp.dma_start(xs_v[:, :, 0:D], x1keep[:, :, :]).then_inc(S["xs_out"], 16)

            with sp.Fori(0, GT // 2) as q:
                pair(q * 2, True, False)
            sp.wait_ge(S["dots"], 2 * NT)
            sp.wait_ge(S["st_zero"], 1)
            sp.dma_start(xs_v[:, :, D:XW], st[:, :, :]).then_inc(S["xs_out"], 16)
            with nc.allow_non_contiguous_dma(reason="8192 values of t, once"):
                sp.dma_start(trow.rearrange("(t p o) -> p t o", p=P, o=1), st[:, :, 0:1])\
                  .then_inc(S["xs_out"], 16)
            sp.wait_ge(S["xs_out"], 48)
            own_x(0)
            sp.wait_ge(S["scattered"], 16 * GT)
            own_x(1)
            for b in range(2):
                load_lists(b, b)
            with sp.Fori(0, (LAG - GT) // 2) as q:
                pair(q * 2 + GT, True, False)
            with sp.Fori((LAG - GT) // 2, GT // 2) as q:
                pair(q * 2 + GT, True, True)
            with sp.Fori(2, NG - 1) as g:
                sp.wait_ge(S["scattered"], g * (16 * GT))
                own_x(g)
                with sp.Fori(0, GT // 2) as q:
                    pair(g * GT + q * 2, True, True)
            sp.wait_ge(S["scattered"], 16 * (NT - GT))
            own_x(NG - 1)
            with sp.Fori(NT // 2 - GT // 2, NT // 2 - 1) as q:
                pair(q * 2, True, True)
            pair(NT - 2, True, True, last=True)
            sp.wait_ge(S["scattered"], 16 * NT)
            with sp.Fori(0, LAG // 2 - 1) as q:
                pair(q * 2 + NT, False, True)

            sp.wait_ge(S["flags_done"], 1)
            any_bad = sp.value_load(flags[0:1, NT:NT + 1], min_val=0, max_val=N)
            with sp.If(any_bad > 0):
                all_scattered(sp, rows_scattered)
                with sp.Fori(0, NT) as t:
                    dense_loads(sp, t, 0, 0)
            with sp.Else():
                sp.nop()

            all_scattered(sp, rows_scattered)
            for b in range(2):
                load_lists(b, b)
            with sp.Fori(0, NT // 2 - 1) as q:
                for b in range(2):
                    sp.wait_ge(S["step_b"], NT + 2 * q + b + 1)
                    load_lists(2 * q + 2 + b, b)

            with sp.If(any_bad > 0):
                all_scattered(sp, out_scattered)
                with sp.Fori(0, NT) as t:
                    dense_loads(sp, t, 1, NT)
            with sp.Else():
                sp.nop()

        @block.gpsimd
        def _(pool):
            pool.iota(iota16[:, :], pattern=[[1, N]], base=1, channel_multiplier=0).then_inc(S["iota_done"], 1)
            pool.memset(ident[:, :], 0.0).then_inc(S["ident_zero"], 1)
            pool.wait_ge(S["ident_zero"], 1)
            pool.affine_select(out=ident[:, :], in_=ident[:, :], compare_op=ALU.not_equal, fill=1.0,
                               base=0, pattern=[[-1, P]], channel_multiplier=1).then_inc(S["ident_done"], 1)
            pool.memset(ones[:, :], 1.0).then_inc(S["ones_done"], 1)
            pool.iota(slot_no[:, :], pattern=[[1, SLOTS]], base=0, channel_multiplier=0,
                      allow_small_or_imprecise_dtypes=True).then_inc(S["consts_done"], 1)
            pool.iota(own_c[:, :], pattern=[[P, GT]], base=0, channel_multiplier=1,
                      allow_small_or_imprecise_dtypes=True).then_inc(S["consts_done"], 1)
            pool.iota(order_c[:, :], pattern=[[-P, GT]], base=GT * P - 1, channel_multiplier=-1,
                      allow_small_or_imprecise_dtypes=True).then_inc(S["consts_done"], 1)
            pool.memset(gbase[:, :], 0.0).then_inc(S["consts_done"], 1)
            pool.memset(epsb[:, :], EPS).then_inc(S["consts_done"], 1)
            pool.memset(st[:, :, 2:4], 0.0).then_inc(S["st_zero"], 1)
            pool.wait_ge(S["x_in"], 16)
            pool.wait_ge(S["attn_in"], 16)
            for k, half in enumerate((1, 0)):
                prod = G[:, k, :, :].rearrange("p s w -> p (s w)")[:, 0:N].rearrange("p (t d) -> p t d", d=D)
                a = attn_b[:, half * D:(half + 1) * D].unsqueeze(1).to_broadcast([P, NT, D])
                pool.tensor_tensor(prod, x1keep[:, :, :], a, ALU.mult).then_inc(S["products"], 1)
            pool.wait_ge(S["dots"], 2 * NT)
            for b in range(2):
                pool.memset(G[:, b, :, D:XW], 0.0).then_inc(S["g_zero"], 1)
            pool.wait_ge(S["g_zero"], 2)

            def gathers(layer, table, width, b, tiles_before):
                held(pool, "pad_pool", lists_in[b], 16 * (tiles_before + 1))
                K = pool.value_load(lp[0:1, b, DEG:DEG + 1], min_val=0, max_val=SLOTS)
                for c in range(NCH):
                    def chunk():
                        for k in range(c * CH, c * CH + CH):
                            pool.indirect_dma_start(
                                out=G[:, b, k, 0:width], out_offset=None, in_=table,
                                in_offset=bass.IndirectOffsetOnAxis(ap=lp[:, b, k:k + 1], axis=0))\
                                .then_inc(gathered[layer][b], 16)
                    if c < BASE_CH:
                        chunk()
                    else:
                        with pool.If(K > c * CH):
                            chunk()
                        with pool.Else():
                            pool.inc_swdge_sem([gathered[layer][b]], [16 * CH], mode="add")

            def scatter_rows(table, b, n, done):
                held(pool, "pad_pool", S["step_c"], n + 1)
                pool.indirect_dma_start(
                    out=table, out_offset=bass.IndirectOffsetOnAxis(ap=own_o[:, b, 0:1], axis=0),
                    in_=rows_o[:, b, :], in_offset=None).then_inc(done, 16)

            def scatter_lists(g):
                pool.wait_ge(S["placed"], g + 1)
                held(pool, "pad_pool", S["own_x"], 16 * (g + 1))
                for t in range(GT):
                    pool.indirect_dma_start(
                        out=lists, out_offset=bass.IndirectOffsetOnAxis(ap=place[:, t:t + 1], axis=0),
                        in_=lists_g[:, t, :], in_offset=None).then_inc(S["scattered"], 16)

            def tile_pair(h, first=False, scatter=None):
                for b in range(2):
                    if scatter is not None and b == 1:
                        scatter_lists(scatter)
                    gathers(0, xs, XW, b, h)
                    if not first:
                        scatter_rows(x1, b, 2 * h + b - 2, rows_scattered[b])

            scatter_lists(0)
            tile_pair(0, first=True)
            with pool.Fori(1, GT // 2 - 1) as q:
                tile_pair(q)
            tile_pair(GT // 2 - 1, scatter=1)
            with pool.Fori(1, NG - 1) as g:
                with pool.Fori(0, GT // 2 - 1) as q:
                    tile_pair(g * (GT // 2) + q)
                tile_pair(g * (GT // 2) + GT // 2 - 1, scatter=g + 1)
            with pool.Fori(NT // 2 - GT // 2, NT // 2) as q:
                tile_pair(q)
            for b in range(2):
                scatter_rows(x1, b, NT - 2 + b, rows_scattered[b])

            all_scattered(pool, rows_scattered)
            pool.wait_ge(S["flags_done"], 1)
            any_bad = pool.value_load(flags[0:1, NT:NT + 1], min_val=0, max_val=N)
            with pool.If(any_bad > 0):
                pool.wait_ge(S["d_stored"], 16 * NT)
            with pool.Else():
                pool.nop()

            def tile_pair_1(q, first=False):
                for b in range(2):
                    gathers(1, x1, D, b, NT // 2 + q)
                    if not first:
                        scatter_rows(out, b, NT + 2 * q + b - 2, out_scattered[b])
            tile_pair_1(0, first=True)
            with pool.Fori(1, NT // 2) as q:
                tile_pair_1(q)
            for b in range(2):
                scatter_rows(out, b, 2 * NT - 2 + b, out_scattered[b])
            all_scattered(pool, out_scattered)

        @block.scalar
        def _(act):
            def signs(i, u):
                if not (isinstance(i, int) and i < 2):
                    act.wait_ge(S["segments"], i - 1)
                for h in range(2):
                    act.wait_ge(adj_in[h], 16 * (i + 1))
                    act.activation(nz[:, u, h * H:(h + 1) * H], adjb[:, h, :], ACT.Sign)\
                       .then_inc(S["signed"], 1)
                    act.wait_ge(S["signed"], 2 * i + h + 1)
                    if not (isinstance(i, int) and i < 2):
                        act.wait_ge(S["listed"], i - 1)
                    act.activation(adjb[:, h, :].bitcast(I16)[:, 0:H], nz[:, u, h * H:(h + 1) * H],
                                   ACT.Square, accum_out=halves[:, u, h:h + 1]).then_inc(S["squared"], 1)

            def dots(i0):
                for k in range(2):
                    prod = G[:, k, :, :].rearrange("p s w -> p (s w)")
                    for dt in range(8):
                        act.activation(stj[:, :], prod[:, bass.ds((i0 + dt) * D, D)], ACT.Copy,
                                       accum_out=st[:, bass.ds(i0 + dt, 1), k:k + 1]
                                       .rearrange("p a b -> p (a b)")).then_inc(S["dots"], 1)
                        act.wait_ge(S["dots"], i0 * 2 + (k * 8 + dt + 1))

            def pair(i0, extract, layer):
                for u in range(2):
                    i = i0 + u
                    if layer:
                        j = i - LAG
                        act.wait_ge(S["step_a"], j + 1)
                        act.activation(w[:, u, :], e[:, :], ACT.Exp, bias=nmax[:, u:u + 1],
                                       accum_out=wsum[:, u:u + 1]).then_inc(S["exped"], 1)
                    if extract:
                        with act.If(i < NT - 1):
                            signs(i + 1, 1 - u)
                        with act.Else():
                            act.nop()
                    if layer:
                        act.wait_ge(S["step_b"], j + 1)
                        act.activation(root[:, u:u + 1], mv[:, u, 1:2], ACT.Sqrt, bias=epsb[:, :])\
                           .then_inc(S["rooted"], 1)

            signs(0, 0)
            act.wait_ge(S["consts_done"], 5)
            act.wait_ge(S["products"], 2)
            signs(1, 1)
            dots(0)
            dots(8)
            with act.Fori(1, GT // 2) as q:
                for u in range(2):
                    signs(q * 2 + u, u)
                    dots(q * 16 + u * 8)
            signs(GT, 0)
            with act.Fori(0, (LAG - GT) // 2) as q:
                pair(q * 2 + GT, True, False)
            with act.Fori((LAG - GT) // 2, GT // 2) as q:
                pair(q * 2 + GT, True, True)
            with act.Fori(2, NG) as g:
                with act.Fori(0, GT // 2) as q:
                    pair(g * GT + q * 2, True, True)
            with act.Fori(0, LAG // 2) as q:
                pair(q * 2 + NT, False, True)

            def dense_points(t, layer, n):
                mark = act.value_load(flags[0:1, bass.ds(t, 1)], min_val=0, max_val=P)
                held(act, "pad_act", S["d_pen"], n + 1)
                with act.If(mark > 0):
                    if layer == 0:
                        act.activation(E, E, ACT.Exp, bias=nmax[:, 0:1], accum_out=wsum[:, 0:1])\
                           .then_inc(S["d_exp"], 1)
                    else:
                        act.sem_inc(S["d_exp"], 1)
                with act.Else():
                    act.sem_inc(S["d_exp"], 1)
                held(act, "pad_act", S["d_var"], n + 1)
                with act.If(mark > 0):
                    act.activation(root[:, 0:1], mv[:, 0, 1:2], ACT.Sqrt, bias=epsb[:, :])\
                       .then_inc(S["d_root"], 1)
                with act.Else():
                    act.sem_inc(S["d_root"], 1)

            act.wait_ge(S["flags_done"], 1)
            any_bad = act.value_load(flags[0:1, NT:NT + 1], min_val=0, max_val=N)
            with act.If(any_bad > 0):
                with act.Fori(0, NT) as t:
                    dense_points(t, 0, t)
            with act.Else():
                act.nop()
            with act.Fori(0, NT // 2) as q:
                for u in range(2):
                    act.wait_ge(S["step_b"], NT + 2 * q + u + 1)
                    act.activation(root[:, u:u + 1], mv[:, u, 1:2], ACT.Sqrt, bias=epsb[:, :])\
                       .then_inc(S["rooted"], 1)
            with act.If(any_bad > 0):
                with act.Fori(0, NT) as t:
                    dense_points(t, 1, t + NT)
            with act.Else():
                act.nop()

        @block.tensor
        def _(pe):
            pe.wait_ge(S["ones_done"], 1)
            half_w = GT * P // 2
            dflat = diag[:, :, :].rearrange("p t c -> p (t c)")
            with pe.Fori(0, NG) as g:
                pe.wait_ge(S["diag_done"], g + 1)
                for h in range(2):
                    pe.matmul(keys_ps[:, h * half_w:(h + 1) * half_w], ones[:, :],
                              dflat[:, h * half_w:(h + 1) * half_w], start=True, stop=True)\
                      .then_inc(S["keys_done"], 1)
            pe.wait_ge(S["placed"], NG)
            pe.matmul(flag_ps[:, :], ones[:, :], bad[:, :], start=True, stop=True).then_inc(S["flags_mm"], 1)

        @block.vector
        def _(dve):
            tick = {"n": 0}

            def begin():
                tick["n"] = 0
                dve.sem_clear(S["fresh"])

            def ready(ins, by=1):
                ins.then_inc(S["fresh"], 1)
                tick["n"] += 1
                dve.wait_ge(S["fresh"], tick["n"])

            def layer_a(h, b):
                begin()
                dve.wait_ge(lists_in[b], 16 * (h + 1))
                dve.wait_ge(gathered[0][b], 16 * SLOTS * (h + 1))
                own = lp[:, b, XAT:].bitcast(F32)
                ready(dve.tensor_copy(degf[:, b:b + 1], lp[:, b, DEG:DEG + 1]))
                ready(dve.tensor_scalar(hide[:, :], slot_no[:, :], degf[:, b:b + 1], FAR, ALU.is_ge, ALU.mult))
                ready(dve.scalar_tensor_tensor(out=z[:, :], in0=G[:, b, :, TCOL], scalar=own[:, SCOL:SCOL + 1],
                                               in1=hide[:, :], op0=ALU.add, op1=ALU.add))
                ready(dve.scalar_tensor_tensor(out=e[:, :], in0=z[:, :], scalar=SLOPE, in1=z[:, :],
                                               op0=ALU.mult, op1=ALU.max))
                ready(dve.tensor_reduce(nmax[:, b:b + 1], e[:, :], AX.X, ALU.max, negate=True))
                dve.sem_inc(S["step_a"], 1)

            def norm_end(b, n, free, keep=None):
                begin()
                dve.wait_ge(S["rooted"], n + 1)
                ready(dve.reciprocal(rstd[:, :], root[:, b:b + 1]))
                if free is not None:
                    dve.wait_ge(*free)
                ready(dve.tensor_scalar(rows_o[:, b, :], y[:, b, :], mv[:, b, 0:1], rstd[:, :],
                                        ALU.subtract, ALU.mult))
                if keep is not None:
                    ready(dve.tensor_copy(keep, rows_o[:, b, :]))
                dve.sem_inc(S["step_c"], 1)

            def layer_b(j, b, free):
                begin()
                dve.sem_clear(S["slot_done"])
                held(dve, "pad_dve", S["exped"], j + 1)
                K = dve.value_load(lp[0:1, b, DEG:DEG + 1], min_val=0, max_val=SLOTS)
                for c in range(NCH):
                    def chunk():
                        for k in range(CH):
                            s = c * CH + k
                            if c == 0:
                                ins = dve.tensor_scalar(acc[:, k, :], G[:, b, s, 0:D], w[:, b, s:s + 1],
                                                        None, ALU.mult)
                            else:
                                dve.wait_ge(S["slot_done"], s - CH + 1)
                                ins = dve.scalar_tensor_tensor(
                                    out=acc[:, k, :], in0=G[:, b, s, 0:D], scalar=w[:, b, s:s + 1],
                                    in1=acc[:, k, :], op0=ALU.mult, op1=ALU.add)
                            ins.then_inc(S["slot_done"], 1)
                    if c < BASE_CH:
                        chunk()
                    else:
                        with dve.If(K > c * CH):
                            chunk()
                        with dve.Else():
                            dve.sem_inc(S["slot_done"], CH)
                dve.wait_ge(S["slot_done"], SLOTS)
                ready(dve.tensor_reduce(agg[:, :], acc[:, :, :].rearrange("p c d -> p d c"), AX.X, ALU.add))
                ready(dve.tensor_scalar(wsafe[:, :], wsum[:, b:b + 1], 1e-30, None, ALU.max))
                ready(dve.reciprocal(wrec[:, :], wsafe[:, :]))
                own = lp[:, b, XAT:].bitcast(F32)
                ready(dve.scalar_tensor_tensor(out=y[:, b, :], in0=agg[:, :], scalar=wrec[:, :],
                                               in1=own[:, 0:D], op0=ALU.mult, op1=ALU.add))
                if free is not None:
                    dve.wait_ge(*free)
                ready(dve.tensor_copy(own_o[:, b, 0:1], lp[:, b, OWN:OWN + 1]))
                ready(dve.bn_stats(stats[:, :], y[:, b, :]))
                ready(dve.bn_aggr(mv[:, b, :], stats[:, :]))
                dve.sem_inc(S["step_b"], 1)

            def extract(i, u, t, lists_free):
                begin()
                dve.sem_clear(S["picked"])
                dve.wait_ge(S["squared"], 2 * i + 2)
                ready(dve.tensor_tensor(nz[:, u, :], nz[:, u, :], iota16[:, :], ALU.mult))
                best = comb[:, 8:].rearrange("p (r s) -> p r s", s=NSEG)
                for s in range(NSEG):
                    dve.max(best[:, :, s], nz[:, u, s * SEG:(s + 1) * SEG]).then_inc(S["picked"], 1)
                dve.wait_ge(S["picked"], NSEG)
                dve.sem_inc(S["segments"], 1)
                ready(dve.max(comb[:, 0:8], comb[:, 8 + HEAD:]))
                for r in range(SLOTS // 8):
                    ready(dve.max(found_l[:, 8 * r:8 * r + 8], comb[:, 0:8 + HEAD]))
                    if r < SLOTS // 8 - 1:
                        ready(dve.match_replace(comb[:, 0:8 + HEAD], found_l[:, 8 * r:8 * r + 8],
                                                comb[:, 0:8 + HEAD], 0.0))
                ready(dve.tensor_scalar(junk[:, :], found_l[:, :], 0.0, None, ALU.is_gt, ALU.add,
                                        accum_out=found[:, bass.ds(t, 1)]))
                ready(dve.tensor_tensor(count[:, :], halves[:, u, 0:1], halves[:, u, 1:2], ALU.add))
                dve.sem_inc(S["listed"], 1)
                ready(dve.tensor_tensor(miss[:, 0:1], count[:, :], found[:, bass.ds(t, 1)], ALU.not_equal))
                ready(dve.tensor_scalar(miss[:, 1:2], found[:, bass.ds(t, 1)], 0.0, None, ALU.is_equal))
                ready(dve.tensor_tensor(bad[:, bass.ds(i, 1)], miss[:, 0:1], miss[:, 1:2], ALU.max))
                ready(dve.tensor_scalar(fill[:, :], found_l[:, :], 0.0, found_l[:, 0:1], ALU.is_equal, ALU.mult))
                ready(dve.tensor_tensor(fill[:, :], fill[:, :], found_l[:, :], ALU.add))
                if lists_free is not None:
                    dve.wait_ge(S["scattered"], lists_free)
                def lg(a, b_):
                    return lists_g[:, bass.ds(t, 1), a:b_].rearrange("p a b -> p (a b)")
                ready(dve.tensor_scalar(lg(0, SLOTS), fill[:, :], 1.0, -1.0, ALU.max, ALU.add))
                ready(dve.tensor_copy(lg(DEG, DEG + 1), found[:, bass.ds(t, 1)]))
                ready(dve.tensor_scalar(lg(OWN, OWN + 1), own_c[:, bass.ds(t, 1)], gbase[:, :], None, ALU.add))
                ready(dve.tensor_copy(lg(OWN + 1, XAT), miss[:, :]))

            def sort(g):
                begin()
                ready(dve.scalar_tensor_tensor(out=key[:, :], in0=found[:, :], scalar=float(GT * P),
                                               in1=order_c[:, :], op0=ALU.mult, op1=ALU.add))
                dve.tensor_tensor(diag[:, :, :], ident[:, :].unsqueeze(1).to_broadcast([P, GT, P]),
                                  key[:, :].unsqueeze(2).to_broadcast([P, GT, P]), ALU.mult)\
                   .then_inc(S["diag_done"], 1)
                dve.wait_ge(S["keys_done"], 2 * (g + 1))
                for t in range(GT):
                    ready(dve.tensor_scalar(diag[:, :, :].rearrange("p t c -> p (t c)"), keys_ps[:, :],
                                            key[:, t:t + 1], None, ALU.is_gt, ALU.add,
                                            accum_out=rank[:, t:t + 1]))
                ready(dve.tensor_scalar(place[:, :], rank[:, :], gbase[:, :], None, ALU.add))
                dve.sem_inc(S["placed"], 1)
                ready(dve.tensor_scalar(gbase[:, :], gbase[:, :], float(GT * P), None, ALU.add))


            def pair(i0, do_extract, do_layer, t0=None, h=None, lists_free=None, first=False):
                for u in range(2):
                    i = i0 + u
                    if do_layer:
                        j = i - LAG
                        layer_a(h, u)
                        if not (first and u == 0):
                            norm_end(1 - u, j - 1,
                                     None if first else (rows_scattered[1 - u], 16 * (h - 1 + u)),
                                     keep=x1keep[:, bass.ds(j - 1, 1), :].rearrange("p a d -> p (a d)"))
                    if do_extract:
                        extract(i, u, t0 + u, lists_free)
                    if do_layer:
                        layer_b(j, u, None if first else (rows_scattered[u], 16 * h))

            dve.wait_ge(S["ident_done"], 1)
            dve.wait_ge(S["iota_done"], 1)
            dve.wait_ge(S["consts_done"], 5)
            with dve.Fori(0, GT // 2) as q:
                pair(q * 2, True, False, q * 2)
            sort(0)
            with dve.Fori(0, (LAG - GT) // 2) as q:
                pair(q * 2 + GT, True, False, q * 2, lists_free=16 * GT)
            pair(LAG, True, True, LAG - GT, 0, 16 * GT, first=True)
            with dve.Fori(1, GT - LAG // 2) as h:
                pair(h * 2 + LAG, True, True, h * 2 + LAG - GT, h, 16 * GT)
            sort(1)
            with dve.Fori(2, NG) as g:
                with dve.Fori(0, GT // 2) as q:
                    pair(g * GT + q * 2, True, True, q * 2, g * (GT // 2) + q - LAG // 2, g * (16 * GT))
                sort(g)
            with dve.Fori((NT - LAG) // 2, NT // 2) as h:
                pair(h * 2 + LAG, False, True, h=h)
            norm_end(1, NT - 1, (rows_scattered[1], 16 * (NT // 2 - 1)), keep=x1keep[:, NT - 1, :])

            dve.wait_ge(S["flags_mm"], 1)

            begin()
            ready(dve.tensor_copy(flagf[:, 0:NT], flag_ps[:, :]))
            ready(dve.tensor_reduce(flagf[:, NT:NT + 1], flagf[:, 0:NT], AX.X, ALU.add))
            ready(dve.tensor_copy(flags[:, 0:NT + 1], flagf[:, 0:NT + 1]))
            dve.sem_inc(S["flags_done"], 1)

            def dense(t, layer, n):
                mark = dve.value_load(flags[0:1, bass.ds(t, 1)], min_val=0, max_val=P)
                pen = penalty.bitcast(F32)
                with dve.If(mark > 0):
                    begin()
                    dve.wait_ge(S["d_adj"], 16 * (n + 1))
                    dve.wait_ge(S["d_own"], 16 * (n + 1))
                    if layer == 0:
                        dve.wait_ge(S["d_t"], 16 * (n + 1))
                        ready(dve.tensor_tensor(part, xo, attn_b[:, 0:D], ALU.mult))
                        ready(dve.tensor_reduce(wsafe[:, :], part, AX.X, ALU.add))
                        ready(dve.tensor_scalar(E, E, wsafe[:, :], None, ALU.add))
                        ready(dve.scalar_tensor_tensor(out=E, in0=E, scalar=SLOPE, in1=E,
                                                       op0=ALU.mult, op1=ALU.max))
                        ready(dve.tensor_scalar(pen, penalty, 0.0, NEG, ALU.is_le, ALU.mult))
                        ready(dve.tensor_tensor(E, E, pen, ALU.add))
                        ready(dve.tensor_reduce(nmax[:, 0:1], E, AX.X, ALU.max, negate=True))
                        ready(dve.memset(dacc, 0.0))
                    else:
                        ready(dve.tensor_scalar(pen, penalty, 0.0, FAR, ALU.is_equal, ALU.mult))
                        ready(dve.memset(dacc, FAR))
                with dve.Else():
                    dve.nop()
                dve.sem_inc(S["d_pen"], 1)
                held(dve, "pad_dve", S["d_exp"], n + 1)
                with dve.If(mark > 0):
                    with dve.Fori(0, ND) as c:
                        begin()
                        dve.wait_ge(S["d_rows"], (n * ND + c + 1) * 16)
                        col = (E if layer == 0 else pen)[:, bass.ds(c * DENSE_CH, DENSE_CH)]
                        ready(dve.tensor_tensor(XBv, XBv, col.unsqueeze(2).to_broadcast([P, DENSE_CH, D]),
                                                ALU.mult if layer == 0 else ALU.add))
                        ready(dve.tensor_reduce(part, XBv.rearrange("p j d -> p d j"), AX.X,
                                                ALU.add if layer == 0 else ALU.max))
                        ready(dve.tensor_tensor(dacc, dacc, part, ALU.add if layer == 0 else ALU.max))
                        dve.sem_inc(S["d_used"], 1)
                    begin()
                    if layer == 0:
                        ready(dve.reciprocal(wrec[:, :], wsum[:, 0:1]))
                    else:
                        ready(dve.tensor_reduce(wsafe[:, :], pen, AX.X, ALU.max))
                        ready(dve.tensor_scalar(wrec[:, :], wsafe[:, :], 0.0, None, ALU.is_equal))
                    ready(dve.scalar_tensor_tensor(out=y[:, 0, :], in0=dacc, scalar=wrec[:, :], in1=xo,
                                                   op0=ALU.mult, op1=ALU.add))
                    ready(dve.bn_stats(stats[:, :], y[:, 0, :]))
                    ready(dve.bn_aggr(mv[:, 0, :], stats[:, :]))
                with dve.Else():
                    dve.sem_inc(S["d_used"], ND)
                dve.sem_inc(S["d_var"], 1)
                held(dve, "pad_dve", S["d_root"], n + 1)
                with dve.If(mark > 0):
                    begin()
                    ready(dve.reciprocal(rstd[:, :], root[:, 0:1]))
                    ready(dve.tensor_scalar(rows_o[:, 0, :], y[:, 0, :], mv[:, 0, 0:1], rstd[:, :],
                                            ALU.subtract, ALU.mult))
                with dve.Else():
                    dve.nop()
                dve.sem_inc(S["d_fin"], 1)
                held(dve, "pad_dve", S["d_stored"], 16 * (n + 1))

            any_bad = dve.value_load(flags[0:1, NT:NT + 1], min_val=0, max_val=N)
            with dve.If(any_bad > 0):
                all_scattered(dve, rows_scattered)
                with dve.Fori(0, NT) as t:
                    dense(t, 0, t)
            with dve.Else():
                dve.nop()

            def max_b(j, b, q, first):
                dve.wait_ge(lists_in[b], 16 * (NT // 2 + q + 1))
                dve.wait_ge(gathered[1][b], 16 * SLOTS * (q + 1))
                dve.sem_inc(S["pad_dve"], 1)
                K = dve.value_load(lp[0:1, b, DEG:DEG + 1], min_val=0, max_val=SLOTS)
                begin()
                dve.sem_clear(S["slot_done"])
                for c in range(1, NCH):
                    def chunk():
                        prev = G[:, b, 0:CH, 0:D] if c == 1 else acc[:, :, :]
                        if c > 1:
                            dve.wait_ge(S["slot_done"], (c - 1) * CH)
                        dve.tensor_tensor(acc[:, :, :], G[:, b, c * CH:(c + 1) * CH, 0:D], prev, ALU.max)\
                           .then_inc(S["slot_done"], CH)
                    if c < BASE_CH:
                        chunk()
                    else:
                        with dve.If(K > c * CH):
                            chunk()
                        with dve.Else():
                            dve.sem_inc(S["slot_done"], CH)
                dve.sem_inc(S["slot_done"], CH)
                dve.wait_ge(S["slot_done"], SLOTS)
                ready(dve.tensor_reduce(agg[:, :], acc[:, :, :].rearrange("p c d -> p d c"), AX.X, ALU.max))
                ready(dve.tensor_tensor(y[:, b, :], agg[:, :],
                                        x1keep[:, bass.ds(j, 1), :].rearrange("p a d -> p (a d)"), ALU.add))
                if not first:
                    dve.wait_ge(out_scattered[b], 16 * q)
                ready(dve.tensor_copy(own_o[:, b, 0:1], lp[:, b, OWN:OWN + 1]))
                ready(dve.bn_stats(stats[:, :], y[:, b, :]))
                ready(dve.bn_aggr(mv[:, b, :], stats[:, :]))
                dve.sem_inc(S["step_b"], 1)

            def pair_1(q, first=False):
                for b in range(2):
                    j = q * 2 + b
                    max_b(j, b, q, first)
                    if not (first and b == 0):
                        norm_end(1 - b, NT + j - 1, None if first else (out_scattered[1 - b], 16 * (q - 1 + b)))

            all_scattered(dve, rows_scattered)
            pair_1(0, first=True)
            with dve.Fori(1, NT // 2) as q:
                pair_1(q)
            norm_end(1, 2 * NT - 1, (out_scattered[1], 16 * (NT // 2 - 1)))

            with dve.If(any_bad > 0):
                all_scattered(dve, out_scattered)
                with dve.Fori(0, NT) as t:
                    dense(t, 1, t + NT)
            with dve.Else():
                dve.nop()


_INS = ["x", "adj", "L0_gnn_attn"]


def kernel(**inputs):
    import numpy as _np
    import concourse.bacc as _bacc
    from concourse import mybir as _mybir
    from concourse.bass_utils import run_bass_kernel_spmd as _run

    nc = _bacc.Bacc("TRN2", target_bir_lowering=False, num_devices=1)
    arrays, args = {}, []
    for name in _INS:
        a = _np.ascontiguousarray(inputs[name])
        arrays[f"in_{name}_dram"] = a
        args.append(nc.dram_tensor(f"in_{name}_dram", a.shape, _mybir.dt.from_np(a.dtype), kind="ExternalInput").ap())
    args.append(nc.dram_tensor("out_0_dram", inputs["x"].shape, _mybir.dt.float32, kind="ExternalOutput").ap())
    gnn_kernel(nc, *args)
    r = _run(nc, [arrays], core_ids=[0])
    return r.results[0]["out_0_dram"]
```

```python
import numpy as np
import concourse.bass as bass
from concourse import mybir
from contextlib import ExitStack

F32 = mybir.dt.float32
I32 = mybir.dt.int32
U32 = mybir.dt.uint32
I16 = mybir.dt.int16
ALU = mybir.AluOpType
ACT = mybir.ActivationFunctionType
AX = mybir.AxisListType

P = 128
SLOTS = 64
BASE = 24
ACCS = 4
RING = 8
SEG = 128
GT = 8
LAG = 10
SLOPE, NEG, EPS = 0.2, -1e9, 1e-5
FAR = -3.0e38
DENSE_CH = 64


def gnn_kernel(nc, x, adj, attn, out):
    N, D = x.shape
    NT = N // P
    NG = NT // GT
    H = N // 2
    NSEG = N // SEG
    TCOL, SCOL, XW = D, D + 1, D + 4
    DEG, OWN, XAT = SLOTS, SLOTS + 1, SLOTS + 4
    LW = XAT + XW
    HEAD = 3 * NSEG
    ND = N // DENSE_CH

    xs = nc.dram_tensor("xs", [N, XW], F32).ap()
    trow = nc.dram_tensor("trow", [N], F32).ap()
    x1 = nc.dram_tensor("x1", [N, D], F32).ap()
    lists = nc.dram_tensor("lists", [N, LW], U32).ap()

    with ExitStack() as ctx:
        def sb(name, shape, dt):
            return ctx.enter_context(nc.sbuf_tensor(name, shape, dt))

        def sem(name):
            return ctx.enter_context(nc.semaphore(name))

        adjb = sb("adjb", [P, 2, H], I32)
        nz = sb("nz", [P, 2, N], I16)
        iota16 = sb("iota16", [P, N], I16)
        G = sb("G", [P, 2, SLOTS, XW], F32)
        x1keep = sb("x1keep", [P, NT, D], F32)
        lists_g = sb("lists_g", [P, GT, LW], U32)
        lp = sb("lp", [P, 2, LW], U32)
        comb = sb("comb", [P, 8 + 8 * NSEG], F32)
        found_l = sb("found_l", [P, SLOTS], F32)
        fill = sb("fill", [P, SLOTS], F32)
        junk = sb("junk", [P, SLOTS], F32)
        halves = sb("halves", [P, 2, 2], F32)
        count = sb("count", [P, 1], F32)
        found = sb("found", [P, GT], F32)
        miss = sb("miss", [P, 2], F32)
        bad = sb("bad", [P, NT], F32)
        key = sb("key", [P, GT], F32)
        order_c = sb("order_c", [P, GT], F32)
        own_c = sb("own_c", [P, GT], F32)
        rank = sb("rank", [P, GT], F32)
        rank0 = sb("rank0", [P, GT], F32)
        place = sb("place", [P, GT], U32)
        gbase = sb("gbase", [P, 1], F32)
        diag = sb("diag", [P, GT, P], F32)
        ident = sb("ident", [P, P], F32)
        ones = sb("ones", [P, P], F32)
        slot_no = sb("slot_no", [P, SLOTS], F32)
        attn_b = sb("attn_b", [P, 2 * D], F32)
        st = sb("st", [P, NT, 4], F32)
        degf = sb("degf", [P, 2], F32)
        hide = sb("hide", [P, SLOTS], F32)
        z = sb("z", [P, SLOTS], F32)
        e = sb("e", [P, SLOTS], F32)
        nmax = sb("nmax", [P, 2], F32)
        w = sb("w", [P, 2, SLOTS], F32)
        wsum = sb("wsum", [P, 2], F32)
        wsafe = sb("wsafe", [P, 1], F32)
        wrec = sb("wrec", [P, 1], F32)
        acc = sb("acc", [P, ACCS, D], F32)
        agg = sb("agg", [P, D], F32)
        y = sb("y", [P, 2, D], F32)
        stats = sb("stats", [P, 6], F32)
        mv = sb("mv", [P, 2, 2], F32)
        root = sb("root", [P, 2], F32)
        rstd = sb("rstd", [P, 1], F32)
        rows_o = sb("rows_o", [P, 2, D], F32)
        own_o = sb("own_o", [P, 2, 2], U32)
        epsb = sb("epsb", [P, 1], F32)
        flags = sb("flags", [P, NT + 2], I32)
        flagf = sb("flagf", [P, NT + 2], F32)
        weigh = sb("weigh", [P, RING, P], F32)
        keys_ps = ctx.enter_context(nc.psum_tensor("keys_ps", [P, GT * P], F32))
        agg_ps = [ctx.enter_context(nc.psum_tensor(f"agg_ps{b}", [P, 512], F32)) for b in range(2)]
        flag_ps = ctx.enter_context(nc.psum_tensor("flag_ps", [P, NT], F32))

        S = {n: sem(n) for n in (
            "x_in attn_in adj_in0 adj_in1 own_x lists_in0 lists_in1 gathered0 gathered1 gathered2 gathered3 "
            "iota_done ident_zero ident_done consts_done ones_done products dots st_zero xs_out g_zero signed squared "
            "segments tail_done picked replaced listed base_done diag_done keys_done ranked placed scattered "
            "step_a exped step_b rooted step_c fresh rows_scattered0 rows_scattered1 slot_done flags_mm flags_done "
            "out_scattered0 out_scattered1 "
            "weighed weigh_used summed pad_pe pad_dve pad_pool pad_sp pad_act d_adj d_t d_own d_rows d_used d_stored d_pen d_exp d_var d_root d_fin").split()}
        adj_in = [S["adj_in0"], S["adj_in1"]]
        lists_in = [S["lists_in0"], S["lists_in1"]]
        gathered = [[S["gathered0"], S["gathered1"]], [S["gathered2"], S["gathered3"]]]

        def tile_rows(ap, t):
            return ap[bass.ds(t * P, P), :]

        rows_scattered = [S["rows_scattered0"], S["rows_scattered1"]]
        out_scattered = [S["out_scattered0"], S["out_scattered1"]]

        def held(eng, pad, s, value):
            eng.wait_ge(s, value)
            eng.sem_inc(S[pad], 1)

        def as_needed(eng, K, slot, skip):
            def rest(s):
                with eng.If(K > s):
                    slot(s)
                    if s + 1 < SLOTS:
                        rest(s + 1)
                with eng.Else():
                    skip(s)
            rest(BASE)

        LAST = BASE - 1

        def all_scattered(eng, sems):
            for b in range(2):
                eng.wait_ge(sems[b], 8 * NT)

        block = ctx.enter_context(nc.Block())


        E = G[:, 0, :, :].rearrange("p s w -> p (s w)")[:, 0:N]
        XB = G[:, 1, :, :].rearrange("p s w -> p (s w)")[:, 0:DENSE_CH * D]
        XBv = XB.rearrange("p (j d) -> p j d", d=D)
        penalty = adjb[:, :, :].rearrange("p a b -> p (a b)")
        xo = acc[:, 1, :]
        part = acc[:, 2, :]
        dacc = acc[:, 0, :]

        def dense_loads(sp, t, layer, base):
            n = t + base
            mark = sp.value_load(flags[0:1, bass.ds(t, 1)], min_val=0, max_val=P)
            src, dst = (x, x1) if layer == 0 else (x1, out)
            with sp.If(mark > 0):
                sp.dma_start(penalty, tile_rows(adj, t)).then_inc(S["d_adj"], 16)
                sp.dma_start(xo, tile_rows(src, t)).then_inc(S["d_own"], 16)
                if layer == 0:
                    sp.dma_start(E, trow.partition_broadcast(P)).then_inc(S["d_t"], 16)
                else:
                    sp.sem_inc(S["d_t"], 16)
                with sp.Fori(0, ND) as c:
                    sp.wait_ge(S["d_used"], n * ND + c)
                    sp.dma_start(XB, src[bass.ds(c * DENSE_CH, DENSE_CH), :]
                                 .rearrange("j d -> (j d)").partition_broadcast(P)).then_inc(S["d_rows"], 16)
            with sp.Else():
                for s, k in (("d_adj", 1), ("d_own", 1), ("d_t", 1), ("d_rows", ND)):
                    sp.sem_inc(S[s], 16 * k)
            held(sp, "pad_sp", S["d_fin"], n + 1)
            with sp.If(mark > 0):
                sp.dma_start(tile_rows(dst, t), rows_o[:, 0, :]).then_inc(S["d_stored"], 16)
            with sp.Else():
                sp.sem_inc(S["d_stored"], 16)
            held(sp, "pad_sp", S["d_stored"], 16 * (n + 1))

        @block.sync
        def _(sp):
            for h in range(2):
                sp.dma_start(adjb[:, h, :], adj[0:P, h * H:(h + 1) * H]).then_inc(adj_in[h], 16)
            sp.dma_start(x1keep[:, :, :], x.rearrange("(t p) d -> p t d", p=P)).then_inc(S["x_in"], 16)
            sp.dma_start(attn_b[:, :], attn.rearrange("d o -> (o d)").partition_broadcast(P))\
              .then_inc(S["attn_in"], 16)

            def load_lists(j, b):
                sp.dma_start(lp[:, b, :], tile_rows(lists, j)).then_inc(lists_in[b], 16)

            def next_half(i, h):
                sp.wait_ge(S["squared"], 2 * i + h + 1)
                sp.dma_start(adjb[:, h, :], tile_rows(adj, i + 1)[:, h * H:(h + 1) * H])\
                  .then_inc(adj_in[h], 16)

            def pair(i0, extract, layer, last=False):
                for u in range(2):
                    i = i0 + u
                    if extract and not (last and u == 1):
                        for h in range(2):
                            next_half(i, h)
                    if layer:
                        j = i - LAG
                        sp.wait_ge(S["step_b"], j + 1)
                        load_lists(j + 2, u)

            def own_x(g):
                sp.dma_start(lists_g[:, :, XAT:].bitcast(F32),
                             xs[bass.ds(g * GT * P, GT * P), :].rearrange("(t p) w -> p t w", p=P))\
                  .then_inc(S["own_x"], 16)

            sp.wait_ge(S["x_in"], 16)
            xs_v = xs.rearrange("(t p) w -> p t w", p=P)
            sp.dma_start(xs_v[:, :, 0:D], x1keep[:, :, :]).then_inc(S["xs_out"], 16)

            pair(0, True, False)
            sp.wait_ge(S["dots"], 2)
            sp.wait_ge(S["st_zero"], 1)
            sp.dma_start(xs_v[:, :, D:XW], st[:, :, :]).then_inc(S["xs_out"], 16)
            with nc.allow_non_contiguous_dma(reason="8192 values of t, once"):
                sp.dma_start(trow.rearrange("(t p o) -> p t o", p=P, o=1), st[:, :, 0:1])\
                  .then_inc(S["xs_out"], 16)
            sp.wait_ge(S["xs_out"], 48)
            own_x(0)
            with sp.Fori(1, GT // 2) as q:
                pair(q * 2, True, False)
            sp.wait_ge(S["scattered"], 16 * GT)
            own_x(1)
            for b in range(2):
                load_lists(b, b)
            with sp.Fori(0, (LAG - GT) // 2) as q:
                pair(q * 2 + GT, True, False)
            with sp.Fori((LAG - GT) // 2, GT // 2) as q:
                pair(q * 2 + GT, True, True)
            with sp.Fori(2, NG - 1) as g:
                sp.wait_ge(S["scattered"], g * (16 * GT))
                own_x(g)
                with sp.Fori(0, GT // 2) as q:
                    pair(g * GT + q * 2, True, True)
            sp.wait_ge(S["scattered"], 16 * (NT - GT))
            own_x(NG - 1)
            with sp.Fori(NT // 2 - GT // 2, NT // 2 - 1) as q:
                pair(q * 2, True, True)
            pair(NT - 2, True, True, last=True)
            sp.wait_ge(S["scattered"], 16 * NT)
            with sp.Fori(0, LAG // 2 - 1) as q:
                pair(q * 2 + NT, False, True)

            sp.wait_ge(S["flags_done"], 1)
            any_bad = sp.value_load(flags[0:1, NT:NT + 1], min_val=0, max_val=N)
            with sp.If(any_bad > 0):
                all_scattered(sp, rows_scattered)
                with sp.Fori(0, NT) as t:
                    dense_loads(sp, t, 0, 0)
            with sp.Else():
                sp.nop()

            all_scattered(sp, rows_scattered)
            for b in range(2):
                load_lists(b, b)
            with sp.Fori(0, NT // 2 - 1) as q:
                for b in range(2):
                    sp.wait_ge(S["step_b"], NT + 2 * q + b + 1)
                    load_lists(2 * q + 2 + b, b)

            with sp.If(any_bad > 0):
                all_scattered(sp, out_scattered)
                with sp.Fori(0, NT) as t:
                    dense_loads(sp, t, 1, NT)
            with sp.Else():
                sp.nop()

        @block.gpsimd
        def _(pool):
            pool.iota(iota16[:, :], pattern=[[1, N]], base=1, channel_multiplier=0).then_inc(S["iota_done"], 1)
            pool.memset(ident[:, :], 0.0).then_inc(S["ident_zero"], 1)
            pool.wait_ge(S["ident_zero"], 1)
            pool.affine_select(out=ident[:, :], in_=ident[:, :], compare_op=ALU.not_equal, fill=1.0,
                               base=0, pattern=[[-1, P]], channel_multiplier=1).then_inc(S["ident_done"], 1)
            pool.memset(ones[:, :], 1.0).then_inc(S["ones_done"], 1)
            pool.iota(slot_no[:, :], pattern=[[1, SLOTS]], base=0, channel_multiplier=0,
                      allow_small_or_imprecise_dtypes=True).then_inc(S["consts_done"], 1)
            pool.iota(own_c[:, :], pattern=[[P, GT]], base=0, channel_multiplier=1,
                      allow_small_or_imprecise_dtypes=True).then_inc(S["consts_done"], 1)
            pool.iota(order_c[:, :], pattern=[[-P, GT]], base=GT * P - 1, channel_multiplier=-1,
                      allow_small_or_imprecise_dtypes=True).then_inc(S["consts_done"], 1)
            pool.memset(gbase[:, :], 0.0).then_inc(S["consts_done"], 1)
            pool.memset(epsb[:, :], EPS).then_inc(S["consts_done"], 1)
            pool.memset(st[:, :, 2:4], 0.0).then_inc(S["st_zero"], 1)
            pool.wait_ge(S["x_in"], 16)
            pool.wait_ge(S["attn_in"], 16)
            for k, half in enumerate((1, 0)):
                prod = G[:, k, :, :].rearrange("p s w -> p (s w)")[:, 0:N].rearrange("p (t d) -> p t d", d=D)
                a = attn_b[:, half * D:(half + 1) * D].unsqueeze(1).to_broadcast([P, NT, D])
                pool.tensor_tensor(prod, x1keep[:, :, :], a, ALU.mult).then_inc(S["products"], 1)
            pool.wait_ge(S["dots"], 2)
            for b in range(2):
                pool.memset(G[:, b, :, D:XW], 0.0).then_inc(S["g_zero"], 1)
            pool.wait_ge(S["g_zero"], 2)

            def gathers(layer, table, width, b, tiles_before, between=None):
                held(pool, "pad_pool", lists_in[b], 16 * (tiles_before + 1))
                K = pool.value_load(lp[0:1, b, DEG:DEG + 1], min_val=0, max_val=SLOTS)

                def gather(k):
                    pool.indirect_dma_start(
                        out=G[:, b, k, 0:width], out_offset=None, in_=table,
                        in_offset=bass.IndirectOffsetOnAxis(ap=lp[:, b, k:k + 1], axis=0))\
                        .then_inc(gathered[layer][b], 16)

                for k in range(BASE):
                    if between is not None and k == BASE * 2 // 3:
                        between()
                    gather(k)
                as_needed(pool, K, gather, lambda s: pool.inc_swdge_sem(
                    [gathered[layer][b]], [16 * (SLOTS - s)], mode="add"))

            def scatter_rows(table, b, n, done):
                held(pool, "pad_pool", S["step_c"], n + 1)
                pool.indirect_dma_start(
                    out=table, out_offset=bass.IndirectOffsetOnAxis(ap=own_o[:, b, 0:1], axis=0),
                    in_=rows_o[:, b, :], in_offset=None).then_inc(done, 16)

            def scatter_lists(g):
                pool.wait_ge(S["placed"], g + 1)
                held(pool, "pad_pool", S["own_x"], 16 * (g + 1))
                for t in range(GT):
                    pool.indirect_dma_start(
                        out=lists, out_offset=bass.IndirectOffsetOnAxis(ap=place[:, t:t + 1], axis=0),
                        in_=lists_g[:, t, :], in_offset=None).then_inc(S["scattered"], 16)

            def tile_pair(h, first=False, scatter=None):
                for b in range(2):
                    gathers(0, xs, XW, b, h,
                            (lambda: scatter_lists(scatter)) if scatter is not None and b == 1 else None)
                    if not first:
                        scatter_rows(x1, b, 2 * h + b - 2, rows_scattered[b])

            scatter_lists(0)
            tile_pair(0, first=True)
            with pool.Fori(1, GT // 2 - 1) as q:
                tile_pair(q)
            tile_pair(GT // 2 - 1, scatter=1)
            with pool.Fori(1, NG - 1) as g:
                with pool.Fori(0, GT // 2 - 1) as q:
                    tile_pair(g * (GT // 2) + q)
                tile_pair(g * (GT // 2) + GT // 2 - 1, scatter=g + 1)
            with pool.Fori(NT // 2 - GT // 2, NT // 2) as q:
                tile_pair(q)
            for b in range(2):
                scatter_rows(x1, b, NT - 2 + b, rows_scattered[b])

            all_scattered(pool, rows_scattered)
            pool.wait_ge(S["flags_done"], 1)
            any_bad = pool.value_load(flags[0:1, NT:NT + 1], min_val=0, max_val=N)
            with pool.If(any_bad > 0):
                pool.wait_ge(S["d_stored"], 16 * NT)
            with pool.Else():
                pool.nop()

            def tile_pair_1(q, first=False):
                for b in range(2):
                    gathers(1, x1, D, b, NT // 2 + q)
                    if not first:
                        scatter_rows(out, b, NT + 2 * q + b - 2, out_scattered[b])
            tile_pair_1(0, first=True)
            with pool.Fori(1, NT // 2) as q:
                tile_pair_1(q)
            for b in range(2):
                scatter_rows(out, b, 2 * NT - 2 + b, out_scattered[b])
            all_scattered(pool, out_scattered)

        @block.scalar
        def _(act):
            def signs(i, u):
                if not (isinstance(i, int) and i < 2):
                    act.wait_ge(S["segments"], i - 1)
                for h in range(2):
                    act.wait_ge(adj_in[h], 16 * (i + 1))
                    act.activation(nz[:, u, h * H:(h + 1) * H], adjb[:, h, :], ACT.Sign)\
                       .then_inc(S["signed"], 1)
                    act.wait_ge(S["signed"], 2 * i + h + 1)
                    if not (isinstance(i, int) and i < 2):
                        act.wait_ge(S["listed"], i - 1)
                    act.activation(adjb[:, h, :].bitcast(I16)[:, 0:H], nz[:, u, h * H:(h + 1) * H],
                                   ACT.Square, accum_out=halves[:, u, h:h + 1]).then_inc(S["squared"], 1)

            def pair(i0, extract, layer):
                for u in range(2):
                    i = i0 + u
                    if layer:
                        j = i - LAG
                        act.wait_ge(S["step_a"], j + 1)
                        act.activation(w[:, u, :], e[:, :], ACT.Exp, bias=nmax[:, u:u + 1],
                                       accum_out=wsum[:, u:u + 1]).then_inc(S["exped"], 1)
                        weigh_tile(j, u)
                    if extract:
                        with act.If(i < NT - 1):
                            signs(i + 1, 1 - u)
                        with act.Else():
                            act.nop()
                    if layer:
                        act.wait_ge(S["step_b"], j + 1)
                        act.activation(root[:, u:u + 1], mv[:, u, 1:2], ACT.Sqrt, bias=epsb[:, :])\
                           .then_inc(S["rooted"], 1)

            def weigh_tile(j, b):
                held(act, "pad_act", S["exped"], j + 1)
                K = act.value_load(lp[0:1, b, DEG:DEG + 1], min_val=0, max_val=SLOTS)

                def slot(s, nth=None):
                    nth = s if nth is None else nth
                    if nth >= RING:
                        act.wait_ge(S["weigh_used"], j * SLOTS + (nth - RING + 1))
                    act.activation(weigh[:, nth % RING, :], ident[:, :], ACT.Copy, scale=w[:, b, s:s + 1])\
                       .then_inc(S["weighed"], 1)

                def end(s):
                    slot(LAST, s - 1)
                    act.wait_ge(S["weighed"], j * SLOTS + s)
                    act.sem_inc(S["weighed"], SLOTS - s)

                for s in range(LAST):
                    slot(s)
                as_needed(act, K, lambda s: slot(s, s - 1), end)
                act.sem_inc(S["pad_act"], 1)

            signs(0, 0)
            act.wait_ge(S["consts_done"], 5)
            signs(1, 1)
            with act.Fori(1, GT // 2) as q:
                for u in range(2):
                    signs(q * 2 + u, u)
            signs(GT, 0)
            with act.Fori(0, (LAG - GT) // 2) as q:
                pair(q * 2 + GT, True, False)
            with act.Fori((LAG - GT) // 2, GT // 2) as q:
                pair(q * 2 + GT, True, True)
            with act.Fori(2, NG) as g:
                with act.Fori(0, GT // 2) as q:
                    pair(g * GT + q * 2, True, True)
            with act.Fori(0, LAG // 2) as q:
                pair(q * 2 + NT, False, True)

            def dense_points(t, layer, n):
                mark = act.value_load(flags[0:1, bass.ds(t, 1)], min_val=0, max_val=P)
                held(act, "pad_act", S["d_pen"], n + 1)
                with act.If(mark > 0):
                    if layer == 0:
                        act.activation(E, E, ACT.Exp, bias=nmax[:, 0:1], accum_out=wsum[:, 0:1])\
                           .then_inc(S["d_exp"], 1)
                    else:
                        act.sem_inc(S["d_exp"], 1)
                with act.Else():
                    act.sem_inc(S["d_exp"], 1)
                held(act, "pad_act", S["d_var"], n + 1)
                with act.If(mark > 0):
                    act.activation(root[:, 0:1], mv[:, 0, 1:2], ACT.Sqrt, bias=epsb[:, :])\
                       .then_inc(S["d_root"], 1)
                with act.Else():
                    act.sem_inc(S["d_root"], 1)

            act.wait_ge(S["flags_done"], 1)
            any_bad = act.value_load(flags[0:1, NT:NT + 1], min_val=0, max_val=N)
            with act.If(any_bad > 0):
                with act.Fori(0, NT) as t:
                    dense_points(t, 0, t)
            with act.Else():
                act.nop()
            with act.Fori(0, NT // 2) as q:
                for u in range(2):
                    act.wait_ge(S["step_b"], NT + 2 * q + u + 1)
                    act.activation(root[:, u:u + 1], mv[:, u, 1:2], ACT.Sqrt, bias=epsb[:, :])\
                       .then_inc(S["rooted"], 1)
            with act.If(any_bad > 0):
                with act.Fori(0, NT) as t:
                    dense_points(t, 1, t + NT)
            with act.Else():
                act.nop()

        @block.tensor
        def _(pe):
            pe.wait_ge(S["ones_done"], 1)
            half_w = GT * P // 2
            dflat = diag[:, :, :].rearrange("p t c -> p (t c)")

            def keys(g):
                pe.wait_ge(S["diag_done"], g + 1)
                for h in range(2):
                    pe.matmul(keys_ps[:, h * half_w:(h + 1) * half_w], ones[:, :],
                              dflat[:, h * half_w:(h + 1) * half_w], start=True, stop=True)\
                      .then_inc(S["keys_done"], 1)

            def sum_tile(j, b):
                held(pe, "pad_pe", S["weighed"], j * SLOTS + 1)
                K = pe.value_load(lp[0:1, b, DEG:DEG + 1], min_val=0, max_val=SLOTS)

                def slot(s, nth=None, stop=False):
                    nth = s if nth is None else nth
                    pe.wait_ge(S["weighed"], j * SLOTS + (nth + 1))
                    pe.matmul(agg_ps[b][:, 0:D], weigh[:, nth % RING, :], G[:, b, s, 0:D],
                              start=(nth == 0), stop=stop).then_inc(S["weigh_used"], 1)

                def end(s):
                    slot(LAST, s - 1, True)
                    pe.wait_ge(S["weigh_used"], j * SLOTS + s)
                    pe.sem_inc(S["weigh_used"], SLOTS - s)

                for s in range(LAST):
                    slot(s)
                as_needed(pe, K, lambda s: slot(s, s - 1), end)
                pe.sem_inc(S["summed"], 1)

            def sum_tiles(lo, hi):
                with pe.Fori(lo, hi) as h:
                    for b in range(2):
                        sum_tile(h * 2 + b, b)

            keys(0)
            sum_tiles(0, GT - LAG // 2)
            keys(1)
            with pe.Fori(2, NG) as g:
                with pe.Fori(0, GT // 2) as q:
                    for b in range(2):
                        sum_tile(g * GT + q * 2 + b - LAG, b)
                keys(g)
            pe.wait_ge(S["placed"], NG)
            pe.matmul(flag_ps[:, :], ones[:, :], bad[:, :], start=True, stop=True).then_inc(S["flags_mm"], 1)
            sum_tiles((NT - LAG) // 2, NT // 2)

        @block.vector
        def _(dve):
            tick = {"n": 0}

            def begin():
                tick["n"] = 0
                dve.sem_clear(S["fresh"])

            def ready(ins, by=1):
                ins.then_inc(S["fresh"], 1)
                tick["n"] += 1
                dve.wait_ge(S["fresh"], tick["n"])

            def layer_a(h, b):
                begin()
                dve.wait_ge(lists_in[b], 16 * (h + 1))
                dve.wait_ge(gathered[0][b], 16 * SLOTS * (h + 1))
                own = lp[:, b, XAT:].bitcast(F32)
                ready(dve.tensor_copy(degf[:, b:b + 1], lp[:, b, DEG:DEG + 1]))
                ready(dve.tensor_scalar(hide[:, :], slot_no[:, :], degf[:, b:b + 1], FAR, ALU.is_ge, ALU.mult))
                ready(dve.scalar_tensor_tensor(out=z[:, :], in0=G[:, b, :, TCOL], scalar=own[:, SCOL:SCOL + 1],
                                               in1=hide[:, :], op0=ALU.add, op1=ALU.add))
                ready(dve.scalar_tensor_tensor(out=e[:, :], in0=z[:, :], scalar=SLOPE, in1=z[:, :],
                                               op0=ALU.mult, op1=ALU.max))
                ready(dve.tensor_reduce(nmax[:, b:b + 1], e[:, :], AX.X, ALU.max, negate=True))
                dve.sem_inc(S["step_a"], 1)

            def norm_end(b, n, free, keep=None):
                begin()
                dve.wait_ge(S["rooted"], n + 1)
                ready(dve.reciprocal(rstd[:, :], root[:, b:b + 1]))
                if free is not None:
                    dve.wait_ge(*free)
                ready(dve.tensor_scalar(rows_o[:, b, :], y[:, b, :], mv[:, b, 0:1], rstd[:, :],
                                        ALU.subtract, ALU.mult))
                if keep is not None:
                    ready(dve.tensor_copy(keep, rows_o[:, b, :]))
                dve.sem_inc(S["step_c"], 1)

            def layer_b(j, b, free):
                begin()
                dve.wait_ge(S["exped"], j + 1)
                ready(dve.tensor_scalar(wsafe[:, :], wsum[:, b:b + 1], 1e-30, None, ALU.max))
                ready(dve.reciprocal(wrec[:, :], wsafe[:, :]))
                own = lp[:, b, XAT:].bitcast(F32)
                dve.wait_ge(S["summed"], j + 1)
                ready(dve.scalar_tensor_tensor(out=y[:, b, :], in0=agg_ps[b][:, 0:D], scalar=wrec[:, :],
                                               in1=own[:, 0:D], op0=ALU.mult, op1=ALU.add))
                if free is not None:
                    dve.wait_ge(*free)
                ready(dve.tensor_copy(own_o[:, b, 0:1], lp[:, b, OWN:OWN + 1]))
                ready(dve.bn_stats(stats[:, :], y[:, b, :]))
                ready(dve.bn_aggr(mv[:, b, :], stats[:, :]))
                dve.sem_inc(S["step_b"], 1)

            def extract(i, u):
                begin()
                dve.sem_clear(S["picked"])
                dve.wait_ge(S["squared"], 2 * i + 2)
                ready(dve.tensor_tensor(nz[:, u, :], nz[:, u, :], iota16[:, :], ALU.mult))
                best = comb[:, 8:].rearrange("p (r s) -> p r s", s=NSEG)
                for s in range(NSEG):
                    dve.max(best[:, :, s], nz[:, u, s * SEG:(s + 1) * SEG]).then_inc(S["picked"], 1)
                dve.wait_ge(S["picked"], NSEG)
                dve.sem_inc(S["segments"], 1)
                ready(dve.max(comb[:, 0:8], comb[:, 8 + HEAD:]))
                for r in range(SLOTS // 8):
                    ready(dve.max(found_l[:, 8 * r:8 * r + 8], comb[:, 0:8 + HEAD]))
                    if r < SLOTS // 8 - 1:
                        ready(dve.match_replace(comb[:, 0:8 + HEAD], found_l[:, 8 * r:8 * r + 8],
                                                comb[:, 0:8 + HEAD], 0.0))

            def write_lists(i, u, t, lists_free):
                begin()
                ready(dve.tensor_scalar(junk[:, :], found_l[:, :], 0.0, None, ALU.is_gt, ALU.add,
                                        accum_out=found[:, bass.ds(t, 1)]))
                ready(dve.tensor_tensor(count[:, :], halves[:, u, 0:1], halves[:, u, 1:2], ALU.add))
                dve.sem_inc(S["listed"], 1)
                ready(dve.tensor_tensor(miss[:, 0:1], count[:, :], found[:, bass.ds(t, 1)], ALU.not_equal))
                ready(dve.tensor_scalar(miss[:, 1:2], found[:, bass.ds(t, 1)], 0.0, None, ALU.is_equal))
                ready(dve.tensor_tensor(bad[:, bass.ds(i, 1)], miss[:, 0:1], miss[:, 1:2], ALU.max))
                ready(dve.tensor_scalar(fill[:, :], found_l[:, :], 0.0, found_l[:, 0:1], ALU.is_equal, ALU.mult))
                ready(dve.tensor_tensor(fill[:, :], fill[:, :], found_l[:, :], ALU.add))
                if lists_free is not None:
                    dve.wait_ge(S["scattered"], lists_free)
                def lg(a, b_):
                    return lists_g[:, bass.ds(t, 1), a:b_].rearrange("p a b -> p (a b)")
                ready(dve.tensor_scalar(lg(0, SLOTS), fill[:, :], 1.0, -1.0, ALU.max, ALU.add))
                ready(dve.tensor_copy(lg(DEG, DEG + 1), found[:, bass.ds(t, 1)]))
                ready(dve.tensor_scalar(lg(OWN, OWN + 1), own_c[:, bass.ds(t, 1)], gbase[:, :], None, ALU.add))
                ready(dve.tensor_copy(lg(OWN + 1, XAT), miss[:, :]))

            def sort(g):
                begin()
                ready(dve.scalar_tensor_tensor(out=key[:, :], in0=found[:, :], scalar=float(GT * P),
                                               in1=order_c[:, :], op0=ALU.mult, op1=ALU.add))
                dve.tensor_tensor(diag[:, :, :], ident[:, :].unsqueeze(1).to_broadcast([P, GT, P]),
                                  key[:, :].unsqueeze(2).to_broadcast([P, GT, P]), ALU.mult)\
                   .then_inc(S["diag_done"], 1)
                dve.wait_ge(S["keys_done"], 2 * (g + 1))
                for t in range(GT):
                    ready(dve.tensor_scalar(diag[:, :, :].rearrange("p t c -> p (t c)"), keys_ps[:, :],
                                            key[:, t:t + 1], None, ALU.is_gt, ALU.add,
                                            accum_out=rank[:, t:t + 1]))
                ready(dve.tensor_scalar(place[:, :], rank[:, :], gbase[:, :], None, ALU.add))
                dve.sem_inc(S["placed"], 1)
                ready(dve.tensor_scalar(gbase[:, :], gbase[:, :], float(GT * P), None, ALU.add))


            def pair(i0, do_extract, do_layer, t0=None, h=None, lists_free=None, first=False,
                     then_sort=None):
                for u in range(2):
                    i = i0 + u
                    if do_layer:
                        j = i - LAG
                        layer_a(h, u)
                        if not (first and u == 0):
                            norm_end(1 - u, j - 1,
                                     None if first else (rows_scattered[1 - u], 16 * (h - 1 + u)),
                                     keep=x1keep[:, bass.ds(j - 1, 1), :].rearrange("p a d -> p (a d)"))
                    if do_extract:
                        extract(i, u)
                    if do_layer:
                        layer_b(j, u, None if first else (rows_scattered[u], 16 * h))
                    if do_extract:
                        write_lists(i, u, t0 + u, lists_free)
                    if then_sort is not None and u == 1:
                        sort(then_sort)

            def find_bad_tiles():
                dve.wait_ge(S["flags_mm"], 1)

                begin()
                ready(dve.tensor_copy(flagf[:, 0:NT], flag_ps[:, :]))
                ready(dve.tensor_reduce(flagf[:, NT:NT + 1], flagf[:, 0:NT], AX.X, ALU.add))
                ready(dve.tensor_copy(flags[:, 0:NT + 1], flagf[:, 0:NT + 1]))
                dve.sem_inc(S["flags_done"], 1)

            dve.wait_ge(S["ident_done"], 1)
            dve.wait_ge(S["iota_done"], 1)
            dve.wait_ge(S["consts_done"], 5)
            pair(0, True, False, 0)
            dve.wait_ge(S["products"], 2)
            for k in range(2):
                prod = G[:, k, :, :].rearrange("p s w -> p (s w)")[:, 0:N].rearrange("p (t d) -> p t d", d=D)
                dve.tensor_reduce(st[:, :, k], prod, AX.X, ALU.add).then_inc(S["dots"], 1)
            with dve.Fori(1, GT // 2) as q:
                pair(q * 2, True, False, q * 2)
            sort(0)
            with dve.Fori(0, (LAG - GT) // 2) as q:
                pair(q * 2 + GT, True, False, q * 2, lists_free=16 * GT)
            pair(LAG, True, True, LAG - GT, 0, 16 * GT, first=True)
            with dve.Fori(1, GT - LAG // 2 - 1) as h:
                pair(h * 2 + LAG, True, True, h * 2 + LAG - GT, h, 16 * GT)
            pair(2 * GT - 2, True, True, GT - 2, GT - 1 - LAG // 2, 16 * GT, then_sort=1)
            with dve.Fori(2, NG) as g:
                with dve.Fori(0, GT // 2 - 1) as q:
                    pair(g * GT + q * 2, True, True, q * 2, g * (GT // 2) + q - LAG // 2, g * (16 * GT))
                pair(g * GT + GT - 2, True, True, GT - 2, g * (GT // 2) + GT // 2 - 1 - LAG // 2,
                     g * (16 * GT), then_sort=g)
            find_bad_tiles()
            with dve.Fori((NT - LAG) // 2, NT // 2) as h:
                pair(h * 2 + LAG, False, True, h=h)
            norm_end(1, NT - 1, (rows_scattered[1], 16 * (NT // 2 - 1)), keep=x1keep[:, NT - 1, :])

            def dense(t, layer, n):
                mark = dve.value_load(flags[0:1, bass.ds(t, 1)], min_val=0, max_val=P)
                pen = penalty.bitcast(F32)
                with dve.If(mark > 0):
                    begin()
                    dve.wait_ge(S["d_adj"], 16 * (n + 1))
                    dve.wait_ge(S["d_own"], 16 * (n + 1))
                    if layer == 0:
                        dve.wait_ge(S["d_t"], 16 * (n + 1))
                        ready(dve.tensor_tensor(part, xo, attn_b[:, 0:D], ALU.mult))
                        ready(dve.tensor_reduce(wsafe[:, :], part, AX.X, ALU.add))
                        ready(dve.tensor_scalar(E, E, wsafe[:, :], None, ALU.add))
                        ready(dve.scalar_tensor_tensor(out=E, in0=E, scalar=SLOPE, in1=E,
                                                       op0=ALU.mult, op1=ALU.max))
                        ready(dve.tensor_scalar(pen, penalty, 0.0, NEG, ALU.is_le, ALU.mult))
                        ready(dve.tensor_tensor(E, E, pen, ALU.add))
                        ready(dve.tensor_reduce(nmax[:, 0:1], E, AX.X, ALU.max, negate=True))
                        ready(dve.memset(dacc, 0.0))
                    else:
                        ready(dve.tensor_scalar(pen, penalty, 0.0, FAR, ALU.is_equal, ALU.mult))
                        ready(dve.memset(dacc, FAR))
                with dve.Else():
                    dve.nop()
                dve.sem_inc(S["d_pen"], 1)
                held(dve, "pad_dve", S["d_exp"], n + 1)
                with dve.If(mark > 0):
                    with dve.Fori(0, ND) as c:
                        begin()
                        dve.wait_ge(S["d_rows"], (n * ND + c + 1) * 16)
                        col = (E if layer == 0 else pen)[:, bass.ds(c * DENSE_CH, DENSE_CH)]
                        ready(dve.tensor_tensor(XBv, XBv, col.unsqueeze(2).to_broadcast([P, DENSE_CH, D]),
                                                ALU.mult if layer == 0 else ALU.add))
                        ready(dve.tensor_reduce(part, XBv.rearrange("p j d -> p d j"), AX.X,
                                                ALU.add if layer == 0 else ALU.max))
                        ready(dve.tensor_tensor(dacc, dacc, part, ALU.add if layer == 0 else ALU.max))
                        dve.sem_inc(S["d_used"], 1)
                    begin()
                    if layer == 0:
                        ready(dve.reciprocal(wrec[:, :], wsum[:, 0:1]))
                    else:
                        ready(dve.tensor_reduce(wsafe[:, :], pen, AX.X, ALU.max))
                        ready(dve.tensor_scalar(wrec[:, :], wsafe[:, :], 0.0, None, ALU.is_equal))
                    ready(dve.scalar_tensor_tensor(out=y[:, 0, :], in0=dacc, scalar=wrec[:, :], in1=xo,
                                                   op0=ALU.mult, op1=ALU.add))
                    ready(dve.bn_stats(stats[:, :], y[:, 0, :]))
                    ready(dve.bn_aggr(mv[:, 0, :], stats[:, :]))
                with dve.Else():
                    dve.sem_inc(S["d_used"], ND)
                dve.sem_inc(S["d_var"], 1)
                held(dve, "pad_dve", S["d_root"], n + 1)
                with dve.If(mark > 0):
                    begin()
                    ready(dve.reciprocal(rstd[:, :], root[:, 0:1]))
                    ready(dve.tensor_scalar(rows_o[:, 0, :], y[:, 0, :], mv[:, 0, 0:1], rstd[:, :],
                                            ALU.subtract, ALU.mult))
                with dve.Else():
                    dve.nop()
                dve.sem_inc(S["d_fin"], 1)
                held(dve, "pad_dve", S["d_stored"], 16 * (n + 1))

            any_bad = dve.value_load(flags[0:1, NT:NT + 1], min_val=0, max_val=N)
            with dve.If(any_bad > 0):
                all_scattered(dve, rows_scattered)
                with dve.Fori(0, NT) as t:
                    dense(t, 0, t)
            with dve.Else():
                dve.nop()

            def max_b(j, b, q, first):
                dve.wait_ge(lists_in[b], 16 * (NT // 2 + q + 1))
                dve.wait_ge(gathered[1][b], 16 * SLOTS * (q + 1))
                dve.sem_inc(S["pad_dve"], 1)
                K = dve.value_load(lp[0:1, b, DEG:DEG + 1], min_val=0, max_val=SLOTS)
                begin()
                dve.sem_clear(S["slot_done"])
                for k in range(ACCS, BASE, ACCS):
                    if k > ACCS:
                        dve.wait_ge(S["slot_done"], k - ACCS)
                    dve.tensor_tensor(acc[:, :, :], G[:, b, k:k + ACCS, 0:D],
                                      G[:, b, 0:ACCS, 0:D] if k == ACCS else acc[:, :, :], ALU.max)\
                       .then_inc(S["slot_done"], ACCS)

                def larger(k):
                    a = k % ACCS
                    dve.wait_ge(S["slot_done"], max(k - 2 * ACCS + 1, BASE - ACCS))
                    dve.tensor_tensor(acc[:, a, :], G[:, b, k, 0:D], acc[:, a, :], ALU.max)\
                       .then_inc(S["slot_done"], 1)

                as_needed(dve, K, larger, lambda s: dve.sem_inc(S["slot_done"], SLOTS - s))
                dve.sem_inc(S["slot_done"], ACCS)
                dve.wait_ge(S["slot_done"], SLOTS)
                ready(dve.tensor_reduce(agg[:, :], acc[:, :, :].rearrange("p c d -> p d c"), AX.X, ALU.max))
                ready(dve.tensor_tensor(y[:, b, :], agg[:, :],
                                        x1keep[:, bass.ds(j, 1), :].rearrange("p a d -> p (a d)"), ALU.add))
                if not first:
                    dve.wait_ge(out_scattered[b], 16 * q)
                ready(dve.tensor_copy(own_o[:, b, 0:1], lp[:, b, OWN:OWN + 1]))
                ready(dve.bn_stats(stats[:, :], y[:, b, :]))
                ready(dve.bn_aggr(mv[:, b, :], stats[:, :]))
                dve.sem_inc(S["step_b"], 1)

            def pair_1(q, first=False):
                for b in range(2):
                    j = q * 2 + b
                    max_b(j, b, q, first)
                    if not (first and b == 0):
                        norm_end(1 - b, NT + j - 1, None if first else (out_scattered[1 - b], 16 * (q - 1 + b)))

            all_scattered(dve, rows_scattered)
            pair_1(0, first=True)
            with dve.Fori(1, NT // 2) as q:
                pair_1(q)
            norm_end(1, 2 * NT - 1, (out_scattered[1], 16 * (NT // 2 - 1)))

            with dve.If(any_bad > 0):
                all_scattered(dve, out_scattered)
                with dve.Fori(0, NT) as t:
                    dense(t, 1, t + NT)
            with dve.Else():
                dve.nop()


_INS = ["x", "adj", "L0_gnn_attn"]


def kernel(**inputs):
    import numpy as _np
    import concourse.bacc as _bacc
    from concourse import mybir as _mybir
    from concourse.bass_utils import run_bass_kernel_spmd as _run

    nc = _bacc.Bacc("TRN2", target_bir_lowering=False, num_devices=1)
    arrays, args = {}, []
    for name in _INS:
        a = _np.ascontiguousarray(inputs[name])
        arrays[f"in_{name}_dram"] = a
        args.append(nc.dram_tensor(f"in_{name}_dram", a.shape, _mybir.dt.from_np(a.dtype), kind="ExternalInput").ap())
    args.append(nc.dram_tensor("out_0_dram", inputs["x"].shape, _mybir.dt.float32, kind="ExternalOutput").ap())
    gnn_kernel(nc, *args)
    r = _run(nc, [arrays], core_ids=[0])
    return r.results[0]["out_0_dram"]
```

```python
import numpy as np
import concourse.bass as bass
from concourse import mybir
from contextlib import ExitStack

F32 = mybir.dt.float32
I32 = mybir.dt.int32
U32 = mybir.dt.uint32
I16 = mybir.dt.int16
BF16 = mybir.dt.bfloat16
ALU = mybir.AluOpType
ACT = mybir.ActivationFunctionType
AX = mybir.AxisListType

P = 128
SLOTS = 64
BASE = (24, 8)
LOW = 2.0 ** 14
ACCS = 4
RING = 8
SEG = 128
GT = 8
TILE_ORDER = (7, 1, 3, 5, 6, 4, 2, 0)
LAG = 10
SLOPE, NEG, EPS = 0.2, -1e9, 1e-5
FAR = -3.0e38
DENSE_CH = 64


def gnn_kernel(nc, x, adj, attn, out):
    N, D = x.shape
    NT = N // P
    NG = NT // GT
    H = N // 2
    NSEG = N // SEG
    TCOL, SCOL, XW = D, D + 1, D + 2
    DEG, OWN, LOWS, BEST = SLOTS, SLOTS + 1, SLOTS + 2, SLOTS + 4
    XAT = BEST + NSEG // 2
    GRP = 8
    UNIT = NSEG // 2
    UG = UNIT // GRP
    LW = XAT + XW
    HEAD = 3 * NSEG
    ND = N // DENSE_CH

    xs = nc.dram_tensor("xs", [N, XW], F32).ap()
    trow = nc.dram_tensor("trow", [N], F32).ap()
    x1 = nc.dram_tensor("x1", [N, D], F32).ap()
    lists = nc.dram_tensor("lists", [N, LW], U32).ap()
    bests = nc.dram_tensor("bests", [NT, NSEG, P], BF16).ap()

    with ExitStack() as ctx:
        def sb(name, shape, dt):
            return ctx.enter_context(nc.sbuf_tensor(name, shape, dt))

        def sem(name):
            return ctx.enter_context(nc.semaphore(name))

        adjb = sb("adjb", [P, 2, H], I32)
        nz = sb("nz", [P, 2, N], I16)
        iota16 = sb("iota16", [P, N], I16)
        G = sb("G", [P, 2, SLOTS, XW], F32)
        x1keep = sb("x1keep", [P, NT, D], F32)
        lists_g = sb("lists_g", [P, GT, LW], U32)
        lp = sb("lp", [P, 2, LW], U32)
        comb = sb("comb", [P, 8 + 8 * NSEG], F32)
        found_l = sb("found_l", [P, SLOTS], F32)
        fill = sb("fill", [P, SLOTS], F32)
        low_l = sb("low_l", [P, SLOTS], F32)
        junk = sb("junk", [P, SLOTS], F32)
        halves = sb("halves", [P, 2, 2], F32)
        count = sb("count", [P, 1], F32)
        found = sb("found", [P, GT], F32)
        miss = sb("miss", [P, 2], F32)
        bad = sb("bad", [P, NT], F32)
        key = sb("key", [P, GT], F32)
        order_c = sb("order_c", [P, GT], F32)
        own_c = sb("own_c", [P, GT], F32)
        rank = sb("rank", [P, GT], F32)
        place = sb("place", [P, GT], U32)
        turned_place = sb("turned_place", [P, GT], F32)
        shift = sb("shift", [P, GT], F32)
        gbase = sb("gbase", [P, 1], F32)
        diag = sb("diag", [P, GT, P], F32)
        ident = sb("ident", [P, P], F32)
        ones = sb("ones", [P, P], F32)
        slot_no = sb("slot_no", [P, SLOTS], F32)
        attn_b = sb("attn_b", [P, 2 * D], F32)
        degf = sb("degf", [P, 2], F32)
        e = sb("e", [P, SLOTS], F32)
        nmax = sb("nmax", [P, 2], F32)
        w = sb("w", [P, 2, SLOTS], F32)
        wsum = sb("wsum", [P, 2], F32)
        wsafe = sb("wsafe", [P, 1], F32)
        wrec = sb("wrec", [P, 1], F32)
        wm = sb("wm", [P, RING + ACCS, P], F32)
        weigh = wm[:, 0:RING, :]
        gmax = wm[:, 0:RING, :]
        acc = wm[:, RING:RING + ACCS, :]
        lowf = sb("lowf", [P, 2], F32)
        lows = sb("lows", [P, NT], F32)
        klow = sb("klow", [P, 1], F32)
        klows = sb("klows", [P, NT], I32)
        best_l = sb("best_l", [P, NSEG], F32)
        seg0 = sb("seg0", [P, NSEG], F32)
        minus_place = sb("minus_place", [P, 1], F32)
        ident_b = sb("ident_b", [P, P], BF16)
        best_t = sb("best_t", [NSEG, 2, P], BF16)
        absent = sb("absent", [P, 2, NSEG], BF16)
        far_b = sb("far_b", [P, P], BF16)
        y = sb("y", [P, 2, D], F32)
        stats = sb("stats", [P, 6], F32)
        mv = sb("mv", [P, 2, 2], F32)
        root = sb("root", [P, 2], F32)
        rstd = sb("rstd", [P, 1], F32)
        rows_o = sb("rows_o", [P, 2, D], F32)
        own_o = sb("own_o", [P, 2, 2], U32)
        epsb = sb("epsb", [P, 1], F32)
        flags = sb("flags", [P, NT + 2], I32)
        st = diag[:, 4, :].rearrange("p (t k) -> p t k", k=2)
        flagf = diag[:, 1, :]
        agg = diag[:, 2, :]
        hide, z = junk, fill
        ps = ctx.enter_context(nc.psum_tensor("ps", [P, 8 * 512], F32))
        keys_ps = ps[:, 0:GT * P]
        agg_ps = [ps[:, 1024:1536], ps[:, 1536:2048]]
        flag_ps = ps[:, 2048:2048 + NT]
        best_ps = [ps[0:NSEG, 2560:2560 + P], ps[0:NSEG, 3072:3072 + P]]
        klow_ps = ps[:, 3584:3584 + P]
        picked_ps = [ps[:, k * 1024:(k + 1) * 1024] for k in range(UG)]
        x1_high = adjb[:, 0, :].bitcast(BF16)
        x1_mid = adjb[:, 1, :].bitcast(BF16)
        x1_low = iota16[:, :].bitcast(BF16)
        x1_raw = G[:, 1, :, :].rearrange("p s w -> p (s w)")[:, 0:N]
        hot = nz[:, :, :].rearrange("p a b -> p (a b)").bitcast(BF16)\
            .rearrange("p (k n) -> p k n", k=4)

        S = {n: sem(n) for n in (
            "x_in attn_in adj_in0 adj_in1 own_x lists_in0 lists_in1 gathered0 gathered1 gathered2 gathered3 "
            "iota_done ident_zero ident_done consts_done ones_done products dots xs_out g_zero signed squared "
            "segments picked listed diag_done keys_done placed scattered "
            "step_a exped step_b rooted step_c fresh rows_scattered0 rows_scattered1 slot_done flags_mm flags_done "
            "out_scattered0 out_scattered1 "
            "turned best_ready best_out0 best_out1 lows_set klow_ps1 klow_diag klow_ps2 klow_done raw_in split_act split_dve "
            "distances best_in0 best_in1 best_in2 best_in3 onehot absent_set group_full group_used "
            "weighed weigh_used summed pad_pe pad_dve pad_pool pad_sp pad_act d_adj d_t d_own d_rows d_used d_stored d_pen d_exp d_var d_root d_fin").split()}
        adj_in = [S["adj_in0"], S["adj_in1"]]
        best_out = [S["best_out0"], S["best_out1"]]
        best_in = [S[f"best_in{k}"] for k in range(4)]
        lists_in = [S["lists_in0"], S["lists_in1"]]
        gathered = [[S["gathered0"], S["gathered1"]], [S["gathered2"], S["gathered3"]]]

        def tile_rows(ap, t):
            return ap[bass.ds(t * P, P), :]

        rows_scattered = [S["rows_scattered0"], S["rows_scattered1"]]
        out_scattered = [S["out_scattered0"], S["out_scattered1"]]

        def held(eng, pad, s, value):
            eng.wait_ge(s, value)
            eng.sem_inc(S[pad], 1)

        def as_needed(eng, K, slot, skip, base):
            def rest(s):
                with eng.If(K > s):
                    slot(s)
                    if s + 1 < SLOTS:
                        rest(s + 1)
                with eng.Else():
                    skip(s)
            rest(base)

        LAST = BASE[0] - 1

        def all_scattered(eng, sems):
            for b in range(2):
                eng.wait_ge(sems[b], 8 * NT)

        block = ctx.enter_context(nc.Block())


        E = G[:, 0, :, :].rearrange("p s w -> p (s w)")[:, 0:N]
        XB = G[:, 1, :, :].rearrange("p s w -> p (s w)")[:, 0:DENSE_CH * D]
        XBv = XB.rearrange("p (j d) -> p j d", d=D)
        penalty = adjb[:, :, :].rearrange("p a b -> p (a b)")
        xo = acc[:, 1, :]
        part = acc[:, 2, :]
        dacc = acc[:, 0, :]

        def dense_loads(sp, t, layer, base):
            n = t + base
            mark = sp.value_load(flags[0:1, bass.ds(t, 1)], min_val=0, max_val=P)
            src, dst = (x, x1) if layer == 0 else (x1, out)
            with sp.If(mark > 0):
                sp.dma_start(penalty, tile_rows(adj, t)).then_inc(S["d_adj"], 16)
                sp.dma_start(xo, tile_rows(src, t)).then_inc(S["d_own"], 16)
                if layer == 0:
                    sp.dma_start(E, trow.partition_broadcast(P)).then_inc(S["d_t"], 16)
                else:
                    sp.sem_inc(S["d_t"], 16)
                with sp.Fori(0, ND) as c:
                    sp.wait_ge(S["d_used"], n * ND + c)
                    sp.dma_start(XB, src[bass.ds(c * DENSE_CH, DENSE_CH), :]
                                 .rearrange("j d -> (j d)").partition_broadcast(P)).then_inc(S["d_rows"], 16)
            with sp.Else():
                for s, k in (("d_adj", 1), ("d_own", 1), ("d_t", 1), ("d_rows", ND)):
                    sp.sem_inc(S[s], 16 * k)
            held(sp, "pad_sp", S["d_fin"], n + 1)
            with sp.If(mark > 0):
                sp.dma_start(tile_rows(dst, t), rows_o[:, 0, :]).then_inc(S["d_stored"], 16)
            with sp.Else():
                sp.sem_inc(S["d_stored"], 16)
            held(sp, "pad_sp", S["d_stored"], 16 * (n + 1))

        @block.sync
        def _(sp):
            for h in range(2):
                sp.dma_start(adjb[:, h, :], adj[0:P, h * H:(h + 1) * H]).then_inc(adj_in[h], 16)
            sp.dma_start(x1keep[:, :, :], x.rearrange("(t p) d -> p t d", p=P)).then_inc(S["x_in"], 16)
            sp.dma_start(attn_b[:, :], attn.rearrange("d o -> (o d)").partition_broadcast(P))\
              .then_inc(S["attn_in"], 16)

            def load_lists(j, b):
                sp.dma_start(lp[:, b, :], tile_rows(lists, j)).then_inc(lists_in[b], 16)

            def next_half(i, h):
                sp.wait_ge(S["squared"], 2 * i + h + 1)
                sp.dma_start(adjb[:, h, :], tile_rows(adj, i + 1)[:, h * H:(h + 1) * H])\
                  .then_inc(adj_in[h], 16)

            def pair(i0, extract, layer, last=False):
                for u in range(2):
                    i = i0 + u
                    if extract and not (last and u == 1):
                        for h in range(2):
                            next_half(i, h)
                    if layer:
                        j = i - LAG
                        sp.wait_ge(S["step_b"], j + 1)
                        load_lists(j + 2, u)
                        store_best(j, u)

            def store_best(j, b):
                sp.wait_ge(S["best_ready"], j + 1)
                sp.dma_start(bests[bass.ds(j, 1), :, :].rearrange("a s p -> (a s) p"), best_t[:, b, :])\
                  .then_inc(best_out[b], 16)

            def own_x(g):
                sp.dma_start(lists_g[:, :, XAT:].bitcast(F32),
                             xs[bass.ds(g * GT * P, GT * P), :].rearrange("(t p) w -> p t w", p=P))\
                  .then_inc(S["own_x"], 16)

            sp.wait_ge(S["x_in"], 16)
            xs_v = xs.rearrange("(t p) w -> p t w", p=P)
            sp.dma_start(xs_v[:, :, 0:D], x1keep[:, :, :]).then_inc(S["xs_out"], 16)

            pair(0, True, False)
            sp.wait_ge(S["dots"], 2)
            sp.dma_start(xs_v[:, :, D:XW], st[:, :, :]).then_inc(S["xs_out"], 16)
            with nc.allow_non_contiguous_dma(reason="8192 values of t, once"):
                sp.dma_start(trow.rearrange("(t p o) -> p t o", p=P, o=1), st[:, :, 0:1])\
                  .then_inc(S["xs_out"], 16)
            sp.wait_ge(S["xs_out"], 48)
            own_x(0)
            with sp.Fori(1, GT // 2) as q:
                pair(q * 2, True, False)
            sp.wait_ge(S["scattered"], 16 * GT)
            own_x(1)
            for b in range(2):
                load_lists(b, b)
            with sp.Fori(0, (LAG - GT) // 2) as q:
                pair(q * 2 + GT, True, False)
            with sp.Fori((LAG - GT) // 2, GT // 2) as q:
                pair(q * 2 + GT, True, True)
            with sp.Fori(2, NG - 1) as g:
                sp.wait_ge(S["scattered"], g * (16 * GT))
                own_x(g)
                with sp.Fori(0, GT // 2) as q:
                    pair(g * GT + q * 2, True, True)
            sp.wait_ge(S["scattered"], 16 * (NT - GT))
            own_x(NG - 1)
            with sp.Fori(NT // 2 - GT // 2, NT // 2 - 1) as q:
                pair(q * 2, True, True)
            pair(NT - 2, True, True, last=True)
            sp.wait_ge(S["scattered"], 16 * NT)
            with sp.Fori(0, LAG // 2 - 1) as q:
                pair(q * 2 + NT, False, True)
            for b in range(2):
                store_best(NT - 2 + b, b)

            sp.wait_ge(S["flags_done"], 1)
            any_bad = sp.value_load(flags[0:1, NT:NT + 1], min_val=0, max_val=N)
            with sp.If(any_bad > 0):
                all_scattered(sp, rows_scattered)
                with sp.Fori(0, NT) as t:
                    dense_loads(sp, t, 0, 0)
            with sp.Else():
                sp.nop()

            all_scattered(sp, rows_scattered)
            sp.dma_start(x1_raw.rearrange("p (g d) -> p g d", d=D), x1.rearrange("(g p) d -> p g d", p=P))\
              .then_inc(S["raw_in"], 16)
            for b in range(2):
                load_lists(b, b)
                sp.wait_ge(best_out[b], 8 * NT)

            def load_best(j, h, k):
                sp.dma_start(hot[:, k, :], bests[bass.ds(j, 1), h * UNIT:(h + 1) * UNIT, :]
                             .rearrange("a s p -> (a s p)").partition_broadcast(P)).then_inc(best_in[k], 16)

            for k in range(4):
                load_best(k // 2, k % 2, k)
            with sp.Fori(0, NT // 2 - 1) as q:
                for k in range(4):
                    j = 2 * q + k // 2
                    sp.wait_ge(S["group_used"], (2 * j + k % 2 + 1) * UG)
                    load_best(j + 2, k % 2, k)
                    if k % 2:
                        sp.wait_ge(S["step_b"], NT + j + 1)
                        load_lists(j + 2, k // 2)

            with sp.If(any_bad > 0):
                all_scattered(sp, out_scattered)
                with sp.Fori(0, NT) as t:
                    dense_loads(sp, t, 1, NT)
            with sp.Else():
                sp.nop()

        @block.gpsimd
        def _(pool):
            pool.iota(iota16[:, :], pattern=[[1, N]], base=1, channel_multiplier=0).then_inc(S["iota_done"], 1)
            pool.memset(ident[:, :], 0.0).then_inc(S["ident_zero"], 1)
            pool.wait_ge(S["ident_zero"], 1)
            pool.affine_select(out=ident[:, :], in_=ident[:, :], compare_op=ALU.not_equal, fill=1.0,
                               base=0, pattern=[[-1, P]], channel_multiplier=1).then_inc(S["ident_done"], 1)
            pool.memset(ones[:, :], 1.0).then_inc(S["ones_done"], 1)
            pool.iota(slot_no[:, :], pattern=[[1, SLOTS]], base=0, channel_multiplier=0,
                      allow_small_or_imprecise_dtypes=True).then_inc(S["consts_done"], 1)
            pool.iota(own_c[:, :], pattern=[[P, GT]], base=0, channel_multiplier=1,
                      allow_small_or_imprecise_dtypes=True).then_inc(S["consts_done"], 1)
            pool.iota(order_c[:, :], pattern=[[-P, GT]], base=GT * P - 1, channel_multiplier=-1,
                      allow_small_or_imprecise_dtypes=True).then_inc(S["consts_done"], 1)
            pool.iota(seg0[:, :], pattern=[[SEG, NSEG]], base=0, channel_multiplier=0,
                      allow_small_or_imprecise_dtypes=True).then_inc(S["consts_done"], 1)
            pool.iota(minus_place[:, :], pattern=[[0, 1]], base=-1, channel_multiplier=-1,
                      allow_small_or_imprecise_dtypes=True).then_inc(S["consts_done"], 1)
            pool.memset(lowf[:, :], 0.0).then_inc(S["consts_done"], 1)
            pool.memset(lows[:, :], 0.0).then_inc(S["consts_done"], 1)
            pool.memset(gbase[:, :], 0.0).then_inc(S["consts_done"], 1)
            pool.memset(epsb[:, :], EPS).then_inc(S["consts_done"], 1)
            pool.wait_ge(S["x_in"], 16)
            pool.wait_ge(S["attn_in"], 16)
            for k, half in enumerate((1, 0)):
                prod = G[:, k, :, :].rearrange("p s w -> p (s w)")[:, 0:N].rearrange("p (t d) -> p t d", d=D)
                a = attn_b[:, half * D:(half + 1) * D].unsqueeze(1).to_broadcast([P, NT, D])
                pool.tensor_tensor(prod, x1keep[:, :, :], a, ALU.mult).then_inc(S["products"], 1)
            pool.wait_ge(S["dots"], 2)
            for b in range(2):
                pool.memset(G[:, b, :, D:XW], 0.0).then_inc(S["g_zero"], 1)
            pool.wait_ge(S["g_zero"], 2)

            def gathers(layer, table, width, b, tiles_before, between=None, tile=None):
                held(pool, "pad_pool", lists_in[b], 16 * (tiles_before + 1))
                K = pool.value_load(lp[0:1, b, DEG:DEG + 1] if layer == 0 else klows[0:1, bass.ds(tile, 1)],
                                    min_val=0, max_val=SLOTS)

                def gather(k):
                    pool.indirect_dma_start(
                        out=G[:, b, k, 0:width], out_offset=None, in_=table,
                        in_offset=bass.IndirectOffsetOnAxis(ap=lp[:, b, k:k + 1], axis=0))\
                        .then_inc(gathered[layer][b], 16)

                for k in range(BASE[layer]):
                    if between is not None and k == BASE[0] * 2 // 3:
                        between()
                    gather(k)
                as_needed(pool, K, gather, lambda s: pool.inc_swdge_sem(
                    [gathered[layer][b]], [16 * (SLOTS - s)], mode="add"), BASE[layer])

            def scatter_rows(table, b, n, done):
                held(pool, "pad_pool", S["step_c"], n + 1)
                pool.indirect_dma_start(
                    out=table, out_offset=bass.IndirectOffsetOnAxis(ap=own_o[:, b, 0:1], axis=0),
                    in_=rows_o[:, b, :], in_offset=None).then_inc(done, 16)

            def scatter_lists(g):
                pool.wait_ge(S["placed"], g + 1)
                held(pool, "pad_pool", S["own_x"], 16 * (g + 1))
                for t in range(GT):
                    pool.indirect_dma_start(
                        out=lists, out_offset=bass.IndirectOffsetOnAxis(ap=place[:, t:t + 1], axis=0),
                        in_=lists_g[:, t, :], in_offset=None).then_inc(S["scattered"], 16)

            def tile_pair(h, first=False, scatter=None):
                for b in range(2):
                    gathers(0, xs, XW, b, h,
                            (lambda: scatter_lists(scatter)) if scatter is not None and b == 1 else None)
                    if not first:
                        scatter_rows(x1, b, 2 * h + b - 2, rows_scattered[b])

            scatter_lists(0)
            tile_pair(0, first=True)
            with pool.Fori(1, GT // 2 - 1) as q:
                tile_pair(q)
            tile_pair(GT // 2 - 1, scatter=1)
            with pool.Fori(1, NG - 1) as g:
                with pool.Fori(0, GT // 2 - 1) as q:
                    tile_pair(g * (GT // 2) + q)
                tile_pair(g * (GT // 2) + GT // 2 - 1, scatter=g + 1)
            with pool.Fori(NT // 2 - GT // 2, NT // 2) as q:
                tile_pair(q)
            for b in range(2):
                scatter_rows(x1, b, NT - 2 + b, rows_scattered[b])

            all_scattered(pool, rows_scattered)
            pool.wait_ge(S["flags_done"], 1)
            any_bad = pool.value_load(flags[0:1, NT:NT + 1], min_val=0, max_val=N)
            with pool.If(any_bad > 0):
                pool.wait_ge(S["d_stored"], 16 * NT)
            with pool.Else():
                pool.nop()

            pool.wait_ge(S["klow_done"], 1)

            def tile_pair_1(q, first=False):
                for b in range(2):
                    if first and b == 1:
                        pool.wait_ge(S["split_dve"], 4)
                    gathers(1, x1, D, b, NT // 2 + q, tile=2 * q + b)
                    if not first:
                        scatter_rows(out, b, NT + 2 * q + b - 2, out_scattered[b])
            tile_pair_1(0, first=True)
            with pool.Fori(1, NT // 2) as q:
                tile_pair_1(q)
            for b in range(2):
                scatter_rows(out, b, 2 * NT - 2 + b, out_scattered[b])
            all_scattered(pool, out_scattered)

        @block.scalar
        def _(act):
            def signs(i, u):
                if not (isinstance(i, int) and i < 2):
                    act.wait_ge(S["segments"], i - 1)
                for h in range(2):
                    act.wait_ge(adj_in[h], 16 * (i + 1))
                    act.activation(nz[:, u, h * H:(h + 1) * H], adjb[:, h, :], ACT.Sign)\
                       .then_inc(S["signed"], 1)
                    act.wait_ge(S["signed"], 2 * i + h + 1)
                    if not (isinstance(i, int) and i < 2):
                        act.wait_ge(S["listed"], i - 1)
                    act.activation(adjb[:, h, :].bitcast(I16)[:, 0:H], nz[:, u, h * H:(h + 1) * H],
                                   ACT.Square, accum_out=halves[:, u, h:h + 1]).then_inc(S["squared"], 1)

            def pair(i0, extract, layer, h=None):
                for u in range(2):
                    i = i0 + u
                    if layer:
                        j = i - LAG
                        act.wait_ge(S["step_a"], j + 1)
                        act.activation(w[:, u, :], e[:, :], ACT.Exp, bias=nmax[:, u:u + 1],
                                       accum_out=wsum[:, u:u + 1]).then_inc(S["exped"], 1)
                        act.wait_ge(S["turned"], j + 1)
                        if not isinstance(h, int):
                            act.wait_ge(best_out[u], 16 * h)
                        act.activation(best_t[:, u, :], best_ps[u], ACT.Copy).then_inc(S["best_ready"], 1)
                        weigh_tile(j, u)
                    if extract:
                        with act.If(i < NT - 1):
                            signs(i + 1, 1 - u)
                        with act.Else():
                            act.nop()
                    if layer:
                        act.wait_ge(S["step_b"], j + 1)
                        act.activation(root[:, u:u + 1], mv[:, u, 1:2], ACT.Sqrt, bias=epsb[:, :])\
                           .then_inc(S["rooted"], 1)

            def weigh_tile(j, b):
                held(act, "pad_act", S["exped"], j + 1)
                K = act.value_load(lp[0:1, b, DEG:DEG + 1], min_val=0, max_val=SLOTS)

                def slot(s, nth=None):
                    nth = s if nth is None else nth
                    if nth >= RING:
                        act.wait_ge(S["weigh_used"], j * SLOTS + (nth - RING + 1))
                    act.activation(weigh[:, nth % RING, :], ident[:, :], ACT.Copy, scale=w[:, b, s:s + 1])\
                       .then_inc(S["weighed"], 1)

                def end(s):
                    slot(LAST, s - 1)
                    act.wait_ge(S["weighed"], j * SLOTS + s)
                    act.sem_inc(S["weighed"], SLOTS - s)

                for s in range(LAST):
                    slot(s)
                as_needed(act, K, lambda s: slot(s, s - 1), end, BASE[0])
                act.sem_inc(S["pad_act"], 1)

            signs(0, 0)
            act.wait_ge(S["consts_done"], 9)
            signs(1, 1)
            with act.Fori(1, GT // 2) as q:
                for u in range(2):
                    signs(q * 2 + u, u)
            signs(GT, 0)
            with act.Fori(0, (LAG - GT) // 2) as q:
                pair(q * 2 + GT, True, False)
            pair(LAG, True, True, 0)
            with act.Fori(1, GT - LAG // 2) as h:
                pair(h * 2 + LAG, True, True, h)
            with act.Fori(2, NG) as g:
                with act.Fori(0, GT // 2) as q:
                    pair(g * GT + q * 2, True, True, g * (GT // 2) + q - LAG // 2)
            with act.Fori((NT - LAG) // 2, NT // 2) as h:
                pair(h * 2 + LAG, False, True, h)

            def dense_points(t, layer, n):
                mark = act.value_load(flags[0:1, bass.ds(t, 1)], min_val=0, max_val=P)
                held(act, "pad_act", S["d_pen"], n + 1)
                with act.If(mark > 0):
                    if layer == 0:
                        act.activation(E, E, ACT.Exp, bias=nmax[:, 0:1], accum_out=wsum[:, 0:1])\
                           .then_inc(S["d_exp"], 1)
                    else:
                        act.sem_inc(S["d_exp"], 1)
                with act.Else():
                    act.sem_inc(S["d_exp"], 1)
                held(act, "pad_act", S["d_var"], n + 1)
                with act.If(mark > 0):
                    act.activation(root[:, 0:1], mv[:, 0, 1:2], ACT.Sqrt, bias=epsb[:, :])\
                       .then_inc(S["d_root"], 1)
                with act.Else():
                    act.sem_inc(S["d_root"], 1)

            act.wait_ge(S["flags_done"], 1)
            any_bad = act.value_load(flags[0:1, NT:NT + 1], min_val=0, max_val=N)
            with act.If(any_bad > 0):
                with act.Fori(0, NT) as t:
                    dense_points(t, 0, t)
            with act.Else():
                act.nop()
            act.wait_ge(S["raw_in"], 16)
            for k, to in enumerate((x1_high, x1_mid)):
                for c in range(2):
                    if k:
                        act.wait_ge(S["split_dve"], c + 1)
                    act.activation(to[:, c * H:(c + 1) * H], x1_raw[:, c * H:(c + 1) * H], ACT.Copy)\
                       .then_inc(S["split_act"], 1)

            def hot_tile(j, b, turn):
                act.wait_ge(lists_in[b], 16 * (NT // 2 + turn + 1))
                act.activation(absent[:, b, :], lp[:, b, BEST:XAT].bitcast(BF16), ACT.Relu,
                               bias=ones[:, 0:1], scale=-1.0).then_inc(S["absent_set"], 1)
                for h in range(2):
                    k = 2 * b + h
                    act.wait_ge(best_in[k], 16 * (turn + 1))
                    act.activation(hot[:, k, :], hot[:, k, :], ACT.Square, bias=minus_place[:, :])\
                       .then_inc(S["distances"], 1)
                    act.wait_ge(S["distances"], 2 * j + h + 1)
                    act.activation(hot[:, k, :], hot[:, k, :], ACT.Relu, bias=ones[:, 0:1], scale=-1.0)\
                       .then_inc(S["onehot"], 1)

            def pair_1(q, last=False):
                for u in range(2):
                    if not (last and u == 1):
                        hot_tile(2 * q + u + 1, 1 - u, q + u)
                    act.wait_ge(S["step_b"], NT + 2 * q + u + 1)
                    act.activation(root[:, u:u + 1], mv[:, u, 1:2], ACT.Sqrt, bias=epsb[:, :])\
                       .then_inc(S["rooted"], 1)

            hot_tile(0, 0, 0)
            with act.Fori(0, NT // 2 - 1) as q:
                pair_1(q)
            pair_1(NT // 2 - 1, last=True)
            with act.If(any_bad > 0):
                with act.Fori(0, NT) as t:
                    dense_points(t, 1, t + NT)
            with act.Else():
                act.nop()

        @block.tensor
        def _(pe):
            pe.wait_ge(S["ones_done"], 1)
            half_w = GT * P // 2
            dflat = diag[:, :, :].rearrange("p t c -> p (t c)")

            def keys(g):
                pe.wait_ge(S["diag_done"], g + 1)
                for h in range(2):
                    pe.matmul(keys_ps[:, h * half_w:(h + 1) * half_w], ones[:, :],
                              dflat[:, h * half_w:(h + 1) * half_w], start=True, stop=True)\
                      .then_inc(S["keys_done"], 1)

            def sum_tile(j, b):
                pe.wait_ge(S["step_a"], j + 1)
                pe.matmul(best_ps[b], lp[:, b, BEST:XAT].bitcast(BF16), ident_b[:, :],
                          start=True, stop=True).then_inc(S["turned"], 1)
                held(pe, "pad_pe", S["weighed"], j * SLOTS + 1)
                K = pe.value_load(lp[0:1, b, DEG:DEG + 1], min_val=0, max_val=SLOTS)

                def slot(s, nth=None, stop=False):
                    nth = s if nth is None else nth
                    pe.wait_ge(S["weighed"], j * SLOTS + (nth + 1))
                    pe.matmul(agg_ps[b][:, 0:D], weigh[:, nth % RING, :], G[:, b, s, 0:D],
                              start=(nth == 0), stop=stop).then_inc(S["weigh_used"], 1)

                def end(s):
                    slot(LAST, s - 1, True)
                    pe.wait_ge(S["weigh_used"], j * SLOTS + s)
                    pe.sem_inc(S["weigh_used"], SLOTS - s)

                for s in range(LAST):
                    slot(s)
                as_needed(pe, K, lambda s: slot(s, s - 1), end, BASE[0])
                pe.sem_inc(S["summed"], 1)

            def sum_tiles(lo, hi):
                with pe.Fori(lo, hi) as h:
                    for b in range(2):
                        sum_tile(h * 2 + b, b)

            keys(0)
            sum_tiles(0, GT - LAG // 2)
            keys(1)
            with pe.Fori(2, NG) as g:
                with pe.Fori(0, GT // 2) as q:
                    for b in range(2):
                        sum_tile(g * GT + q * 2 + b - LAG, b)
                keys(g)
            pe.wait_ge(S["placed"], NG)
            pe.matmul(flag_ps[:, :], ones[:, :], bad[:, :], start=True, stop=True).then_inc(S["flags_mm"], 1)
            sum_tiles((NT - LAG) // 2, NT // 2)

            pe.wait_ge(S["lows_set"], 1)
            pe.matmul(klow_ps[0:NT, :], lows[:, :], ident[:, :], start=True, stop=True).then_inc(S["klow_ps1"], 1)
            pe.wait_ge(S["klow_diag"], 1)
            pe.matmul(klow_ps[:, 0:NT], ones[0:NT, :], diag[0:NT, 0, 0:NT], start=True, stop=True).then_inc(S["klow_ps2"], 1)

            def pick_tile(j, b, first=False):
                pe.wait_ge(S["absent_set"], j + 1)
                for h in range(2):
                    pe.wait_ge(S["onehot"], 2 * j + h + 1)
                    for q in range(UG):
                        if not (first and h == 0):
                            pe.wait_ge(S["group_used"], (2 * j + h - 1) * UG + q + 1)
                        for r in range(GRP):
                            n = q * GRP + r
                            seg = h * UNIT + n
                            to = picked_ps[q][:, r * P:(r + 1) * P]
                            pe.matmul(to, far_b[:, :], absent[:, b, seg:seg + 1].to_broadcast([P, D]),
                                      start=True, stop=False)
                            for k, part_ in enumerate((x1_high, x1_mid, x1_low)):
                                last = pe.matmul(to, hot[:, 2 * b + h, n * P:(n + 1) * P],
                                                 part_[:, seg * D:(seg + 1) * D], start=False, stop=(k == 2))
                        last.then_inc(S["group_full"], 1)

            pe.wait_ge(S["split_dve"], 4)
            pick_tile(0, 0, first=True)
            pick_tile(1, 1)
            with pe.Fori(1, NT // 2) as q:
                for b in range(2):
                    pick_tile(2 * q + b, b)

        @block.vector
        def _(dve):
            tick = {"n": 0}

            def begin():
                tick["n"] = 0
                dve.sem_clear(S["fresh"])

            def ready(ins, by=1):
                ins.then_inc(S["fresh"], 1)
                tick["n"] += 1
                dve.wait_ge(S["fresh"], tick["n"])

            def layer_a(h, b):
                begin()
                dve.wait_ge(lists_in[b], 16 * (h + 1))
                dve.wait_ge(gathered[0][b], 16 * SLOTS * (h + 1))
                own = lp[:, b, XAT:].bitcast(F32)
                ready(dve.tensor_copy(degf[:, b:b + 1], lp[:, b, DEG:DEG + 1]))
                ready(dve.tensor_copy(lows[:, bass.ds(2 * h + b, 1)], lp[:, b, LOWS:LOWS + 1]))
                ready(dve.tensor_scalar(hide[:, :], slot_no[:, :], degf[:, b:b + 1], FAR, ALU.is_ge, ALU.mult))
                ready(dve.scalar_tensor_tensor(out=z[:, :], in0=G[:, b, :, TCOL], scalar=own[:, SCOL:SCOL + 1],
                                               in1=hide[:, :], op0=ALU.add, op1=ALU.add))
                ready(dve.scalar_tensor_tensor(out=e[:, :], in0=z[:, :], scalar=SLOPE, in1=z[:, :],
                                               op0=ALU.mult, op1=ALU.max))
                ready(dve.tensor_reduce(nmax[:, b:b + 1], e[:, :], AX.X, ALU.max, negate=True))
                dve.sem_inc(S["step_a"], 1)

            def norm_end(b, n, free, keep=None):
                begin()
                dve.wait_ge(S["rooted"], n + 1)
                ready(dve.reciprocal(rstd[:, :], root[:, b:b + 1]))
                if free is not None:
                    dve.wait_ge(*free)
                ready(dve.tensor_scalar(rows_o[:, b, :], y[:, b, :], mv[:, b, 0:1], rstd[:, :],
                                        ALU.subtract, ALU.mult))
                if keep is not None:
                    ready(dve.tensor_copy(keep, rows_o[:, b, :]))
                dve.sem_inc(S["step_c"], 1)

            def layer_b(j, b, free):
                begin()
                dve.wait_ge(S["exped"], j + 1)
                ready(dve.tensor_scalar(wsafe[:, :], wsum[:, b:b + 1], 1e-30, None, ALU.max))
                ready(dve.reciprocal(wrec[:, :], wsafe[:, :]))
                own = lp[:, b, XAT:].bitcast(F32)
                dve.wait_ge(S["summed"], j + 1)
                ready(dve.scalar_tensor_tensor(out=y[:, b, :], in0=agg_ps[b][:, 0:D], scalar=wrec[:, :],
                                               in1=own[:, 0:D], op0=ALU.mult, op1=ALU.add))
                if free is not None:
                    dve.wait_ge(*free)
                ready(dve.tensor_copy(own_o[:, b, 0:1], lp[:, b, OWN:OWN + 1]))
                ready(dve.bn_stats(stats[:, :], y[:, b, :]))
                ready(dve.bn_aggr(mv[:, b, :], stats[:, :]))
                dve.sem_inc(S["step_b"], 1)

            best = comb[:, 8:].rearrange("p (r s) -> p r s", s=NSEG)

            def search_segments(i, u):
                begin()
                dve.sem_clear(S["picked"])
                dve.wait_ge(S["squared"], 2 * i + 2)
                ready(dve.tensor_tensor(nz[:, u, :], nz[:, u, :], iota16[:, :], ALU.mult))
                for s in range(NSEG):
                    dve.max(best[:, :, s], nz[:, u, s * SEG:(s + 1) * SEG]).then_inc(S["picked"], 1)
                dve.wait_ge(S["picked"], NSEG)
                dve.sem_inc(S["segments"], 1)

            def merge_segments():
                begin()
                dve.tensor_tensor(low_l[:, :], comb[:, 8:8 + NSEG], seg0[:, :], ALU.subtract)\
                   .then_inc(S["fresh"], 1)
                tick["n"] += 1
                ready(dve.tensor_scalar(comb[:, 8 + NSEG:], comb[:, 8 + NSEG:], LOW, None, ALU.mult))
                ready(dve.tensor_scalar(best_l[:, :], low_l[:, :], 0.0, None, ALU.max))
                ready(dve.max(comb[:, 0:8], comb[:, 8 + HEAD:]))
                for r in range(SLOTS // 8):
                    ready(dve.max(found_l[:, 8 * r:8 * r + 8], comb[:, 0:8 + HEAD]))
                    if r < SLOTS // 8 - 1:
                        ready(dve.match_replace(comb[:, 0:8 + HEAD], found_l[:, 8 * r:8 * r + 8],
                                                comb[:, 0:8 + HEAD], 0.0))

            def write_lists(i, u, t, lists_free):
                begin()
                ready(dve.tensor_scalar(junk[:, :], found_l[:, :], 0.0, None, ALU.is_gt, ALU.add,
                                        accum_out=found[:, bass.ds(t, 1)]))
                ready(dve.tensor_tensor(count[:, :], halves[:, u, 0:1], halves[:, u, 1:2], ALU.add))
                dve.sem_inc(S["listed"], 1)
                ready(dve.tensor_tensor(miss[:, 0:1], count[:, :], found[:, bass.ds(t, 1)], ALU.not_equal))
                ready(dve.tensor_scalar(miss[:, 1:2], found[:, bass.ds(t, 1)], 0.0, None, ALU.is_equal))
                ready(dve.tensor_tensor(bad[:, bass.ds(i, 1)], miss[:, 0:1], miss[:, 1:2], ALU.max))
                ready(dve.tensor_scalar(junk[:, :], found_l[:, :], float(N), None, ALU.is_gt, ALU.add,
                                        accum_out=lowf[:, 0:1]))
                ready(dve.scalar_tensor_tensor(out=fill[:, :], in0=found_l[:, :], scalar=float(N),
                                               in1=found_l[:, :], op0=ALU.is_le, op1=ALU.mult))
                ready(dve.tensor_tensor(low_l[:, :], found_l[:, :], fill[:, :], ALU.subtract))
                ready(dve.scalar_tensor_tensor(out=found_l[:, :], in0=low_l[:, :], scalar=1.0 / LOW,
                                               in1=fill[:, :], op0=ALU.mult, op1=ALU.add))
                ready(dve.tensor_scalar(fill[:, :], found_l[:, :], 0.0, found_l[:, 0:1], ALU.is_equal, ALU.mult))
                ready(dve.tensor_tensor(fill[:, :], fill[:, :], found_l[:, :], ALU.add))
                if lists_free is not None:
                    dve.wait_ge(S["scattered"], lists_free)
                def lg(a, b_):
                    return lists_g[:, bass.ds(t, 1), a:b_].rearrange("p a b -> p (a b)")
                ready(dve.tensor_scalar(lg(0, SLOTS), fill[:, :], 1.0, -1.0, ALU.max, ALU.add))
                ready(dve.tensor_copy(lg(DEG, DEG + 1), found[:, bass.ds(t, 1)]))
                ready(dve.tensor_scalar(lg(OWN, OWN + 1), own_c[:, bass.ds(t, 1)], gbase[:, :], None, ALU.add))
                ready(dve.tensor_copy(lg(LOWS, BEST), lowf[:, :]))
                ready(dve.tensor_copy(lg(BEST, XAT).bitcast(BF16), best_l[:, :]))

            def sort(g):
                begin()
                ready(dve.scalar_tensor_tensor(out=key[:, :], in0=found[:, :], scalar=float(GT * P),
                                               in1=order_c[:, :], op0=ALU.mult, op1=ALU.add))
                dve.tensor_tensor(diag[:, :, :], ident[:, :].unsqueeze(1).to_broadcast([P, GT, P]),
                                  key[:, :].unsqueeze(2).to_broadcast([P, GT, P]), ALU.mult)\
                   .then_inc(S["diag_done"], 1)
                dve.wait_ge(S["keys_done"], 2 * (g + 1))
                for t in range(GT):
                    ready(dve.tensor_scalar(diag[:, :, :].rearrange("p t c -> p (t c)"), keys_ps[:, :],
                                            key[:, t:t + 1], None, ALU.is_gt, ALU.add,
                                            accum_out=rank[:, t:t + 1]))
                ahead = [turn - t for t, turn in enumerate(TILE_ORDER)]
                ready(dve.tensor_scalar(turned_place[:, :], rank[:, :], gbase[:, :], float(P * ahead[0]),
                                        ALU.add, ALU.add))
                for t in range(1, GT):
                    ready(dve.tensor_scalar(shift[:, :], rank[:, :], float(P * t),
                                            float(P * (ahead[t] - ahead[t - 1])), ALU.is_ge, ALU.mult))
                    ready(dve.tensor_tensor(turned_place[:, :], turned_place[:, :], shift[:, :], ALU.add))
                ready(dve.tensor_copy(place[:, :], turned_place[:, :]))
                dve.sem_inc(S["placed"], 1)
                ready(dve.tensor_scalar(gbase[:, :], gbase[:, :], float(GT * P), None, ALU.add))


            def pair(i0, do_extract, do_layer, t0=None, h=None, lists_free=None, first=False,
                     then_sort=None):
                for u in range(2):
                    i = i0 + u
                    if do_layer:
                        j = i - LAG
                        layer_a(h, u)
                        if not (first and u == 0):
                            norm_end(1 - u, j - 1,
                                     None if first else (rows_scattered[1 - u], 16 * (h - 1 + u)),
                                     keep=x1keep[:, bass.ds(j - 1, 1), :].rearrange("p a d -> p (a d)"))
                    if do_extract:
                        search_segments(i, u)
                    if do_layer:
                        layer_b(j, u, None if first else (rows_scattered[u], 16 * h))
                    if do_extract:
                        merge_segments()
                        write_lists(i, u, t0 + u, lists_free)
                    if then_sort is not None and u == 1:
                        sort(then_sort)

            def find_bad_tiles():
                dve.wait_ge(S["flags_mm"], 1)

                begin()
                ready(dve.tensor_copy(flagf[:, 0:NT], flag_ps[:, :]))
                ready(dve.tensor_reduce(flagf[:, NT:NT + 1], flagf[:, 0:NT], AX.X, ALU.add))
                ready(dve.tensor_copy(flags[:, 0:NT + 1], flagf[:, 0:NT + 1]))
                dve.sem_inc(S["flags_done"], 1)

            dve.wait_ge(S["ident_done"], 1)
            dve.wait_ge(S["iota_done"], 1)
            dve.wait_ge(S["consts_done"], 9)
            begin()
            ready(dve.tensor_copy(ident_b[:, :], ident[:, :]))
            ready(dve.tensor_scalar(far_b[:, :], ident[:, :], FAR, None, ALU.mult))
            pair(0, True, False, 0)
            dve.wait_ge(S["products"], 2)
            for k in range(2):
                prod = G[:, k, :, :].rearrange("p s w -> p (s w)")[:, 0:N].rearrange("p (t d) -> p t d", d=D)
                dve.tensor_reduce(st[:, :, k], prod, AX.X, ALU.add).then_inc(S["dots"], 1)
            with dve.Fori(1, GT // 2) as q:
                pair(q * 2, True, False, q * 2)
            dve.wait_ge(S["xs_out"], 48)
            sort(0)
            with dve.Fori(0, (LAG - GT) // 2) as q:
                pair(q * 2 + GT, True, False, q * 2, lists_free=16 * GT)
            pair(LAG, True, True, LAG - GT, 0, 16 * GT, first=True)
            with dve.Fori(1, GT - LAG // 2 - 1) as h:
                pair(h * 2 + LAG, True, True, h * 2 + LAG - GT, h, 16 * GT)
            pair(2 * GT - 2, True, True, GT - 2, GT - 1 - LAG // 2, 16 * GT, then_sort=1)
            with dve.Fori(2, NG) as g:
                with dve.Fori(0, GT // 2 - 1) as q:
                    pair(g * GT + q * 2, True, True, q * 2, g * (GT // 2) + q - LAG // 2, g * (16 * GT))
                pair(g * GT + GT - 2, True, True, GT - 2, g * (GT // 2) + GT // 2 - 1 - LAG // 2,
                     g * (16 * GT), then_sort=g)
            find_bad_tiles()
            with dve.Fori((NT - LAG) // 2, NT // 2) as h:
                pair(h * 2 + LAG, False, True, h=h)
            norm_end(1, NT - 1, (rows_scattered[1], 16 * (NT // 2 - 1)), keep=x1keep[:, NT - 1, :])

            def dense(t, layer, n):
                mark = dve.value_load(flags[0:1, bass.ds(t, 1)], min_val=0, max_val=P)
                pen = penalty.bitcast(F32)
                with dve.If(mark > 0):
                    begin()
                    dve.wait_ge(S["d_adj"], 16 * (n + 1))
                    dve.wait_ge(S["d_own"], 16 * (n + 1))
                    if layer == 0:
                        dve.wait_ge(S["d_t"], 16 * (n + 1))
                        ready(dve.tensor_tensor(part, xo, attn_b[:, 0:D], ALU.mult))
                        ready(dve.tensor_reduce(wsafe[:, :], part, AX.X, ALU.add))
                        ready(dve.tensor_scalar(E, E, wsafe[:, :], None, ALU.add))
                        ready(dve.scalar_tensor_tensor(out=E, in0=E, scalar=SLOPE, in1=E,
                                                       op0=ALU.mult, op1=ALU.max))
                        ready(dve.tensor_scalar(pen, penalty, 0.0, NEG, ALU.is_le, ALU.mult))
                        ready(dve.tensor_tensor(E, E, pen, ALU.add))
                        ready(dve.tensor_reduce(nmax[:, 0:1], E, AX.X, ALU.max, negate=True))
                        ready(dve.memset(dacc, 0.0))
                    else:
                        ready(dve.tensor_scalar(pen, penalty, 0.0, FAR, ALU.is_equal, ALU.mult))
                        ready(dve.memset(dacc, FAR))
                with dve.Else():
                    dve.nop()
                dve.sem_inc(S["d_pen"], 1)
                held(dve, "pad_dve", S["d_exp"], n + 1)
                with dve.If(mark > 0):
                    with dve.Fori(0, ND) as c:
                        begin()
                        dve.wait_ge(S["d_rows"], (n * ND + c + 1) * 16)
                        col = (E if layer == 0 else pen)[:, bass.ds(c * DENSE_CH, DENSE_CH)]
                        ready(dve.tensor_tensor(XBv, XBv, col.unsqueeze(2).to_broadcast([P, DENSE_CH, D]),
                                                ALU.mult if layer == 0 else ALU.add))
                        ready(dve.tensor_reduce(part, XBv.rearrange("p j d -> p d j"), AX.X,
                                                ALU.add if layer == 0 else ALU.max))
                        ready(dve.tensor_tensor(dacc, dacc, part, ALU.add if layer == 0 else ALU.max))
                        dve.sem_inc(S["d_used"], 1)
                    begin()
                    if layer == 0:
                        ready(dve.reciprocal(wrec[:, :], wsum[:, 0:1]))
                    else:
                        ready(dve.tensor_reduce(wsafe[:, :], pen, AX.X, ALU.max))
                        ready(dve.tensor_scalar(wrec[:, :], wsafe[:, :], 0.0, None, ALU.is_equal))
                    ready(dve.scalar_tensor_tensor(out=y[:, 0, :], in0=dacc, scalar=wrec[:, :], in1=xo,
                                                   op0=ALU.mult, op1=ALU.add))
                    ready(dve.bn_stats(stats[:, :], y[:, 0, :]))
                    ready(dve.bn_aggr(mv[:, 0, :], stats[:, :]))
                with dve.Else():
                    dve.sem_inc(S["d_used"], ND)
                dve.sem_inc(S["d_var"], 1)
                held(dve, "pad_dve", S["d_root"], n + 1)
                with dve.If(mark > 0):
                    begin()
                    ready(dve.reciprocal(rstd[:, :], root[:, 0:1]))
                    ready(dve.tensor_scalar(rows_o[:, 0, :], y[:, 0, :], mv[:, 0, 0:1], rstd[:, :],
                                            ALU.subtract, ALU.mult))
                with dve.Else():
                    dve.nop()
                dve.sem_inc(S["d_fin"], 1)
                held(dve, "pad_dve", S["d_stored"], 16 * (n + 1))

            dve.sem_inc(S["lows_set"], 1)
            dve.wait_ge(S["klow_ps1"], 1)
            begin()
            ready(dve.tensor_reduce(klow[0:NT, :], klow_ps[0:NT, :], AX.X, ALU.max))
            ready(dve.tensor_scalar(diag[0:NT, 0, 0:NT], ident[0:NT, 0:NT], klow[0:NT, :], None, ALU.mult))
            dve.sem_inc(S["klow_diag"], 1)
            dve.wait_ge(S["klow_ps2"], 1)
            ready(dve.tensor_copy(klows[:, :], klow_ps[:, 0:NT]))
            dve.sem_inc(S["klow_done"], 1)

            any_bad = dve.value_load(flags[0:1, NT:NT + 1], min_val=0, max_val=N)
            with dve.If(any_bad > 0):
                all_scattered(dve, rows_scattered)
                with dve.Fori(0, NT) as t:
                    dense(t, 0, t)
            with dve.Else():
                dve.nop()

            def group_maxima(j, h):
                for q in range(UG):
                    dve.wait_ge(S["group_full"], (2 * j + h) * UG + q + 1)
                    dve.tensor_reduce(gmax[:, h * UG + q, :],
                                      picked_ps[q].rearrange("p (s d) -> p d s", d=D), AX.X, ALU.max)\
                       .then_inc(S["group_used"], 1)

            def max_b(j, b, q, first):
                held(dve, "pad_dve", gathered[1][b], 16 * SLOTS * (q + 1))
                K = dve.value_load(klows[0:1, bass.ds(j, 1)], min_val=0, max_val=SLOTS)
                begin()
                dve.sem_clear(S["slot_done"])
                base = BASE[1]
                for k in range(ACCS, base, ACCS):
                    if k > ACCS:
                        dve.wait_ge(S["slot_done"], k - ACCS)
                    dve.tensor_tensor(acc[:, :, :], G[:, b, k:k + ACCS, 0:D],
                                      G[:, b, 0:ACCS, 0:D] if k == ACCS else acc[:, :, :], ALU.max)\
                       .then_inc(S["slot_done"], ACCS)

                def larger(k):
                    a = k % ACCS
                    dve.wait_ge(S["slot_done"], max(k - 2 * ACCS + 1, base - ACCS))
                    dve.tensor_tensor(acc[:, a, :], G[:, b, k, 0:D], acc[:, a, :], ALU.max)\
                       .then_inc(S["slot_done"], 1)

                as_needed(dve, K, larger, lambda s: dve.sem_inc(S["slot_done"], SLOTS - s), base)
                dve.sem_inc(S["slot_done"], ACCS)
                dve.wait_ge(S["slot_done"], SLOTS)
                dve.wait_ge(S["group_used"], (2 * j + 2) * UG)
                ready(dve.tensor_reduce(agg[:, :], wm[:, :, :].rearrange("p c d -> p d c"), AX.X, ALU.max))
                ready(dve.tensor_tensor(y[:, b, :], agg[:, :],
                                        x1keep[:, bass.ds(j, 1), :].rearrange("p a d -> p (a d)"), ALU.add))
                if not first:
                    dve.wait_ge(out_scattered[b], 16 * q)
                ready(dve.tensor_copy(own_o[:, b, 0:1], lp[:, b, OWN:OWN + 1]))
                ready(dve.bn_stats(stats[:, :], y[:, b, :]))
                ready(dve.bn_aggr(mv[:, b, :], stats[:, :]))
                dve.sem_inc(S["step_b"], 1)

            def pair_1(q, first=False):
                for b in range(2):
                    j = q * 2 + b
                    group_maxima(j, 0)
                    group_maxima(j, 1)
                    max_b(j, b, q, first)
                    if not (first and b == 0):
                        norm_end(1 - b, NT + j - 1, None if first else (out_scattered[1 - b], 16 * (q - 1 + b)))

            all_scattered(dve, rows_scattered)
            for k, (of, to) in enumerate(((x1_high, x1_raw), (x1_mid, x1_low))):
                for c in range(2):
                    dve.wait_ge(S["split_act"], 2 * k + c + 1)
                    dve.tensor_tensor(to[:, c * H:(c + 1) * H], x1_raw[:, c * H:(c + 1) * H],
                                      of[:, c * H:(c + 1) * H], ALU.subtract).then_inc(S["split_dve"], 1)
            pair_1(0, first=True)
            with dve.Fori(1, NT // 2) as q:
                pair_1(q)
            norm_end(1, 2 * NT - 1, (out_scattered[1], 16 * (NT // 2 - 1)))

            with dve.If(any_bad > 0):
                all_scattered(dve, out_scattered)
                with dve.Fori(0, NT) as t:
                    dense(t, 1, t + NT)
            with dve.Else():
                dve.nop()


_INS = ["x", "adj", "L0_gnn_attn"]


def kernel(**inputs):
    import numpy as _np
    import concourse.bacc as _bacc
    from concourse import mybir as _mybir
    from concourse.bass_utils import run_bass_kernel_spmd as _run

    nc = _bacc.Bacc("TRN2", target_bir_lowering=False, num_devices=1)
    arrays, args = {}, []
    for name in _INS:
        a = _np.ascontiguousarray(inputs[name])
        arrays[f"in_{name}_dram"] = a
        args.append(nc.dram_tensor(f"in_{name}_dram", a.shape, _mybir.dt.from_np(a.dtype), kind="ExternalInput").ap())
    args.append(nc.dram_tensor("out_0_dram", inputs["x"].shape, _mybir.dt.float32, kind="ExternalOutput").ap())
    gnn_kernel(nc, *args)
    r = _run(nc, [arrays], core_ids=[0])
    return r.results[0]["out_0_dram"]
```
